# Optimizing a Trainium2 kernel written in Bass

```python
import numpy as np
import jax
import jax.numpy as jnp

def _softmax(x, axis=-1):
    return jax.nn.softmax(x, axis=axis)
def _gelu(x):
    return jax.nn.gelu(x, approximate=True)
def _silu(x):
    return jax.nn.silu(x)
def _sigmoid(x):
    return jax.nn.sigmoid(x)
def _layernorm(x, axis=-1, eps=1e-5):
    m = jnp.mean(x, axis=axis, keepdims=True)
    v = jnp.var(x, axis=axis, keepdims=True)
    return (x - m) / jnp.sqrt(v + eps)
def _scatter_add(tgt, idx, src, axis=0):
    return tgt.at[idx].add(src)
def _segment_sum(src, seg, n):
    return jax.ops.segment_sum(src, seg, n)

kernel_name = 'mk_conv_preact_d2_conv_nchw32_0c5461'

def setup_inputs(seed: int = 0):
    np.random.seed(seed)
    _w = jnp.asarray
    def _rec_inputs():
        import jax
        import jax.numpy as jnp
        _gk = jax.random.key(seed)
        x = -0.0005207 + 1.001 * jax.random.normal(jax.random.fold_in(_gk, 1), (16, 32, 64, 64), jnp.float32)
        return x
    x = _rec_inputs()
    def _L0_conv_setup():
        import jax, jax.numpy as jnp
        import numpy as np
        KH, KW = (3, 3)
        STRIDE = (1, 1)
        PAD = (1, 1)
        NUM_ITERATIONS = 3
        EPS = 1e-12

        def squash(s, axis=-1):
            n2 = jnp.sum(s * s, axis=axis, keepdims=True)
            return s * n2 / ((1.0 + n2) * jnp.sqrt(n2 + EPS))

        def extract_patches(x, kh, kw, stride, pad):
            N, C, H, W = x.shape
            xp = jnp.pad(x, ((0, 0), (0, 0), (pad[0], pad[0]), (pad[1], pad[1])))
            Ho = (H + 2 * pad[0] - kh) // stride[0] + 1
            Wo = (W + 2 * pad[1] - kw) // stride[1] + 1
            rows = []
            for i in range(kh):
                cols = []
                for j in range(kw):
                    cols.append(xp[:, :, i:i + stride[0] * Ho:stride[0], j:j + stride[1] * Wo:stride[1]])
                rows.append(jnp.stack(cols, axis=-1))
            return jnp.stack(rows, axis=-2)
        key = jax.random.key(seed)
        k1, k2 = jax.random.split(key)
        x = jax.random.normal(k1, (16, 32, 64, 64), dtype=jnp.float32)
        weight = jax.random.normal(k2, (4, 4, KH, KW, 8, 8), dtype=jnp.float32)
        return {'x': x, 'weight': weight}
    _L0_conv_all = _L0_conv_setup()
    _L0_conv_in = {k: v for k, v in _L0_conv_all.items() if k in ('weight', )}
    del _L0_conv_all

    def _L1_conv_setup():
        import jax, jax.numpy as jnp
        import numpy as np
        NUM_HEADS = 8
        N_CHUNKS = 4
        EPS = 1e-05

        def _ln2(x):
            m = x.mean(axis=(1, 2), keepdims=True)
            v = x.var(axis=(1, 2), keepdims=True)
            return (x - m) / jnp.sqrt(v + EPS)

        def _dmha(x, Wr, Wqkv, Wp, bp):
            B, N, _ = x.shape
            xr = x @ Wr.T
            C2 = xr.shape[-1]
            hd = C2 // NUM_HEADS
            qkv = (xr @ Wqkv.T).reshape(B, N, 3, NUM_HEADS, hd).transpose(2, 0, 3, 1, 4)
            n = N // N_CHUNKS
            q = qkv[0].reshape(B, NUM_HEADS, N_CHUNKS, n, hd)
            k = qkv[1].reshape(B, NUM_HEADS, N_CHUNKS, n, hd)
            v = qkv[2].reshape(B, NUM_HEADS, N_CHUNKS, n, hd)
            scale = hd ** (-0.5)
            attn = jnp.einsum('bhcnd,bhcmd->bhcnm', q, k) * scale
            attn = jax.nn.softmax(attn, axis=-1)
            o = jnp.einsum('bhcnm,bhcmd->bhcnd', attn, v)
            o = o.transpose(0, 2, 3, 1, 4).reshape(B, N, C2)
            return o @ Wp.T + bp

        def _mlp(x, W1, b1, W2, b2):
            h = jax.nn.relu(x @ W1.T + b1)
            return h @ W2.T + b2
        key = jax.random.key(seed)
        ks = jax.random.split(key, 8)
        B, C, H, W = (8, 32, 64, 64)
        dim = C * 9
        c2 = dim // 2
        hid = dim // 4
        s = 0.02
        return {'x': jax.random.normal(ks[0], (B, C, H, W), jnp.float32), 'Wr': jax.random.normal(ks[1], (c2, dim), jnp.float32) * s, 'Wqkv': jax.random.normal(ks[2], (3 * c2, c2), jnp.float32) * s, 'Wp': jax.random.normal(ks[3], (dim, c2), jnp.float32) * s, 'bp': jnp.zeros((dim,), jnp.float32), 'W1': jax.random.normal(ks[4], (hid, dim), jnp.float32) * s, 'b1': jnp.zeros((hid,), jnp.float32), 'W2': jax.random.normal(ks[5], (dim, hid), jnp.float32) * s, 'b2': jnp.zeros((dim,), jnp.float32)}
    _L1_conv_all = _L1_conv_setup()
    _L1_conv_in = {k: v for k, v in _L1_conv_all.items() if k in ('Wr', 'Wqkv', 'Wp', 'bp', 'W1', 'b1', 'W2', 'b2', )}
    del _L1_conv_all

    return {
        "x": x,
        "L0_conv_weight": _L0_conv_in["weight"],
        "L1_conv_Wr": _L1_conv_in["Wr"],
        "L1_conv_Wqkv": _L1_conv_in["Wqkv"],
        "L1_conv_Wp": _L1_conv_in["Wp"],
        "L1_conv_bp": _L1_conv_in["bp"],
        "L1_conv_W1": _L1_conv_in["W1"],
        "L1_conv_b1": _L1_conv_in["b1"],
        "L1_conv_W2": _L1_conv_in["W2"],
        "L1_conv_b2": _L1_conv_in["b2"],
    }

def reference(x, L0_conv_weight, L1_conv_Wr, L1_conv_Wqkv, L1_conv_Wp, L1_conv_bp, L1_conv_W1, L1_conv_b1, L1_conv_W2, L1_conv_b2):
    import jax
    import jax.numpy as jnp
    def _L0_conv_ref(x, weight):
        import jax, jax.numpy as jnp
        import numpy as np
        KH, KW = (3, 3)
        STRIDE = (1, 1)
        PAD = (1, 1)
        NUM_ITERATIONS = 3
        EPS = 1e-12

        def squash(s, axis=-1):
            n2 = jnp.sum(s * s, axis=axis, keepdims=True)
            return s * n2 / ((1.0 + n2) * jnp.sqrt(n2 + EPS))

        def extract_patches(x, kh, kw, stride, pad):
            N, C, H, W = x.shape
            xp = jnp.pad(x, ((0, 0), (0, 0), (pad[0], pad[0]), (pad[1], pad[1])))
            Ho = (H + 2 * pad[0] - kh) // stride[0] + 1
            Wo = (W + 2 * pad[1] - kw) // stride[1] + 1
            rows = []
            for i in range(kh):
                cols = []
                for j in range(kw):
                    cols.append(xp[:, :, i:i + stride[0] * Ho:stride[0], j:j + stride[1] * Wo:stride[1]])
                rows.append(jnp.stack(cols, axis=-1))
            return jnp.stack(rows, axis=-2)
        F_out, F_in, kh, kw, out_len, in_len = weight.shape
        N, C, H, W = x.shape
        patches = extract_patches(x, kh, kw, STRIDE, PAD)
        Ho, Wo = (patches.shape[2], patches.shape[3])
        patches = patches.reshape(N, F_in, in_len, Ho, Wo, kh, kw)
        priors = jnp.einsum('nfdhwij,ofijud->nhwofiju', patches, weight)
        priors = priors.reshape(N, Ho, Wo, F_out, F_in * kh * kw, out_len)
        logits = jnp.zeros_like(priors)
        out = None
        for r in range(NUM_ITERATIONS):
            probs = jax.nn.softmax(logits, axis=-3)
            out = jnp.sum(probs * priors, axis=-2, keepdims=True)
            if r != NUM_ITERATIONS - 1:
                out = squash(out)
                logits = logits + jnp.sum(priors * out, axis=-1, keepdims=True)
        out = squash(jnp.squeeze(out, axis=-2))
        out = out.reshape(N, Ho, Wo, F_out * out_len)
        return jnp.transpose(out, (0, 3, 1, 2))

    def _L1_conv_ref(x, Wr, Wqkv, Wp, bp, W1, b1, W2, b2):
        import jax, jax.numpy as jnp
        import numpy as np
        NUM_HEADS = 8
        N_CHUNKS = 4
        EPS = 1e-05

        def _ln2(x):
            m = x.mean(axis=(1, 2), keepdims=True)
            v = x.var(axis=(1, 2), keepdims=True)
            return (x - m) / jnp.sqrt(v + EPS)

        def _dmha(x, Wr, Wqkv, Wp, bp):
            B, N, _ = x.shape
            xr = x @ Wr.T
            C2 = xr.shape[-1]
            hd = C2 // NUM_HEADS
            qkv = (xr @ Wqkv.T).reshape(B, N, 3, NUM_HEADS, hd).transpose(2, 0, 3, 1, 4)
            n = N // N_CHUNKS
            q = qkv[0].reshape(B, NUM_HEADS, N_CHUNKS, n, hd)
            k = qkv[1].reshape(B, NUM_HEADS, N_CHUNKS, n, hd)
            v = qkv[2].reshape(B, NUM_HEADS, N_CHUNKS, n, hd)
            scale = hd ** (-0.5)
            attn = jnp.einsum('bhcnd,bhcmd->bhcnm', q, k) * scale
            attn = jax.nn.softmax(attn, axis=-1)
            o = jnp.einsum('bhcnm,bhcmd->bhcnd', attn, v)
            o = o.transpose(0, 2, 3, 1, 4).reshape(B, N, C2)
            return o @ Wp.T + bp

        def _mlp(x, W1, b1, W2, b2):
            h = jax.nn.relu(x @ W1.T + b1)
            return h @ W2.T + b2
        B, C, H, W = x.shape
        xp = jnp.pad(x, ((0, 0), (0, 0), (1, 1), (1, 1)))
        pat = jnp.stack([xp[:, :, i:i + H, j:j + W] for i in range(3) for j in range(3)], axis=2)
        t = pat.reshape(B, C * 9, H * W).transpose(0, 2, 1)
        t = t + _dmha(_ln2(t), Wr, Wqkv, Wp, bp)
        t = t + _mlp(_ln2(t), W1, b1, W2, b2)
        y = t.transpose(0, 2, 1).reshape(B, C, 9, H, W)
        out = jnp.zeros((B, C, H + 2, W + 2), x.dtype)
        idx = 0
        for i in range(3):
            for j in range(3):
                out = out.at[:, :, i:i + H, j:j + W].add(y[:, :, idx])
                idx += 1
        return out[:, :, 1:H + 1, 1:W + 1]

    def _gn(v, G=16, eps=1e-5):
        B_, C_, H_, W_ = v.shape
        g = v.reshape(B_, G, C_ // G, H_, W_)
        m = jnp.mean(g, axis=(2, 3, 4), keepdims=True)
        s = jnp.var(g, axis=(2, 3, 4), keepdims=True)
        return ((g - m) / jnp.sqrt(s + eps)).reshape(v.shape)

    def _ln_c(v, eps=1e-6):
        m = jnp.mean(v, axis=1, keepdims=True)
        s = jnp.var(v, axis=1, keepdims=True)
        return (v - m) / jnp.sqrt(s + eps)

    def _ln_t(v, eps=1e-5):
        m = jnp.mean(v, axis=-1, keepdims=True)
        s = jnp.var(v, axis=-1, keepdims=True)
        return (v - m) / jnp.sqrt(s + eps)

    def _to_tokens(v):
        B_, C_, H_, W_ = v.shape
        return v.reshape(B_, C_, H_ * W_).transpose(0, 2, 1)
    def _from_tokens(t, like):
        B_, C_, H_, W_ = like.shape
        return t.transpose(0, 2, 1).reshape(B_, C_, H_, W_)

    x = x + _L0_conv_ref(_gn(x), L0_conv_weight)
    x = x + _L1_conv_ref(_gn(x), L1_conv_Wr, L1_conv_Wqkv, L1_conv_Wp, L1_conv_bp, L1_conv_W1, L1_conv_b1, L1_conv_W2, L1_conv_b2)
    return x


_drawn_inputs = setup_inputs


def setup_inputs(seed=0):
    import zlib

    import numpy as np

    out = dict(_drawn_inputs(seed))
    spreads = {'L1_conv_bp': (0.0, 0.881), 'L1_conv_b1': (0.0, 0.8), 'L1_conv_b2': (0.0, 0.87)}
    factors = {'L1_conv_Wr': 8.0,
     'L1_conv_Wqkv': 8.0,
     'L1_conv_Wp': 8.0,
     'L1_conv_W1': 5.332,
     'L1_conv_W2': 4.152}
    for name, (base, spread) in spreads.items():
        noise = np.random.default_rng([zlib.crc32(name.encode()), seed]).standard_normal(out[name].shape)
        drawn = base * np.exp(spread * noise) if base else spread * noise
        out[name] = jnp.asarray(drawn.astype(out[name].dtype))
    for name, factor in factors.items():
        out[name] = (out[name] * factor).astype(out[name].dtype)
    return out
```

```python
from contextlib import ExitStack

import concourse.bass as bass
import numpy as np
from concourse import mybir

F32 = mybir.dt.float32
BF16 = mybir.dt.bfloat16
ALU = mybir.AluOpType
ACT = mybir.ActivationFunctionType
EXP_LN = "natural_log_exp_and_others"
AX_X = mybir.AxisListType.X

C = 32
IMG = 64
PIX = IMG * IMG
PAD = IMG + 2
TAPS = 9
GN_EPS = 1e-5
LN_EPS = 1e-5
SQUASH_EPS = 1e-12

CAPS, CLEN = 4, 8
LANES = 4
CHUNK = 512
CROWS = CHUNK // IMG
BLK = CHUNK // 128
HALF_ROWS = LANES * CROWS + 2
HALF = HALF_ROWS * PAD
ORDER = [4, 5, 0, 1, 2, 3, 8, 6, 7]
POOLED = {4, 5}
BATCHES = [(0, 1, 2, 3), (8,), (4, 5, 6, 7)]
RINGS = 4

HEADS, HD = 8, 18
DIM, C2, HID = C * TAPS, C * TAPS // 2, C * TAPS // 4


class Signal:

    def __init__(self, sem, per, primed=0):
        self.sem, self.per, self.base = sem, per, per * primed

    def at(self, n, k):
        return n * self.per + (self.base + k)

    def before(self, n, k):
        return n * self.per + (self.base - self.per + k)


def norm_phase(nc, ctx, sems, name, src, add, consts, halves, ln_halves=None, total=None):
    rows = src.shape[0]
    tiles = rows // 128

    def sb(n, shape, dt=F32):
        return ctx.enter_context(nc.sbuf_tensor(f"{name}_{n}", shape, dt))

    def sem(n):
        sems.append(nc.alloc_semaphore(f"{name}_{n}"))
        return sems[-1]

    raw = sb("raw", [128, 2, PIX])
    more = sb("more", [128, 2, PIX]) if add is not None else None
    padded = sb("padded", [128, 2, PAD, PAD])
    pairs = sb("pairs", [128, 128])
    stats = sb("stats", [128, TAPS - 1, 6])
    mv = sb("mv", [128, 2])
    work = sb("work", [128, 12])
    mom = sb("mom", [128, 2])
    ps = ctx.enter_context(nc.psum_tensor(f"{name}_ps", [128, 512], F32))
    if ln_halves is not None:
        sample = sb("sample", [128, 128])
        count = sb("count", [128, PIX])
        weighted = sb("weighted", [128, PIX])
        ln_pad = sb("ln_pad", [128, 2, PAD * PAD])
    loaded = [sem("loaded0"), sem("loaded1")]
    fixed = sem("fixed")
    cleared = sem("cleared")
    chain = sem("chain")
    to_pe = sem("to_pe")
    avg = sem("avg")
    to_act = sem("to_act")
    acted = sem("acted")
    images = sem("images")
    stored = [sem("stored0"), sem("stored1")]
    kept = [sem("kept0"), sem("kept1")]
    mats = 2 if ln_halves is not None else 1
    n_load = 2 if add is not None else 1
    n_ln = ln_halves is not None

    block = ctx.enter_context(nc.Block())
    per_load = 16 * (1 + (4 if add is not None else 0))

    def store(sp, t):
        sp.wait_ge(images, t + 1)
        for s in range(4):
            for h in range(2):
                r0 = h * LANES * CROWS
                rows_of = padded[C * s:C * s + C, t % 2, r0:r0 + HALF_ROWS, :]
                sp.dma_start(halves[8 * t + 2 * s + h, :, :],
                             rows_of.rearrange("p a b -> p (a b)")).then_inc(stored[t % 2], 16)
                if n_ln:
                    sp.dma_start(ln_halves[8 * t + 2 * s + h, :, :],
                                 ln_pad[C * s:C * s + C, t % 2, r0 * PAD:r0 * PAD + HALF]
                                 ).then_inc(stored[t % 2], 16)
        if add is not None:
            sp.dma_start(total[128 * t:128 * t + 128, :], raw[:, t % 2, :]).then_inc(kept[t % 2], 16)

    @block.sync
    def _(sp):
        sp.dma_start(pairs[:, :], consts["pairs"]).then_inc(fixed, 16)
        if n_ln:
            sp.dma_start(sample[:, :], consts["sample"]).then_inc(fixed, 16)
            sp.dma_start(count[:, :], consts["count"].to_broadcast([128, PIX])).then_inc(fixed, 16)
        for t in range(tiles):
            if t >= 2:
                sp.wait_ge(images, t - 1)
                if add is not None:
                    sp.wait_ge(kept[t % 2], 16 * (t // 2))
            sp.dma_start(raw[:, t % 2, :], src[128 * t:128 * t + 128, :]).then_inc(loaded[t % 2], 16)
            if add is not None:
                for s in range(4):
                    to = more[C * s:C * s + C, t % 2, :].rearrange("c (h x) -> c h x", h=2)
                    v = add[8 * t + 2 * s:8 * t + 2 * s + 2, :, :].rearrange("h c x -> c h x")
                    sp.dma_start(to, v).then_inc(loaded[t % 2], 16)
            if t >= 1:
                store(sp, t - 1)
        store(sp, tiles - 1)
        for p in range(2):
            sp.wait_ge(stored[p], 16 * (16 if n_ln else 8) * ((tiles + 1 - p) // 2))
            if add is not None:
                sp.wait_ge(kept[p], 16 * ((tiles + 1 - p) // 2))

    n_avg = 3 if n_ln else 2
    n_to_act = 2 if n_ln else 1
    n_acted = 4 if n_ln else 2

    @block.tensor
    def _(pe):
        pe.wait_ge(fixed, 16 * (1 + 2 * n_ln))
        for t in range(tiles):
            pe.wait_ge(to_pe, n_avg * t + 1)
            pe.matmul(ps[:, 0:2], pairs[:, :], mv[:, :], start=True, stop=True).then_inc(avg, 1)
            pe.wait_ge(to_pe, n_avg * t + 2)
            pe.matmul(ps[:, 0:1], pairs[:, :], work[:, 1:2], start=True, stop=True).then_inc(avg, 1)
            if n_ln:
                pe.wait_ge(to_pe, n_avg * t + 3)
                pe.matmul(ps[:, 0:2], sample[:, :], mom[:, :], start=True, stop=True).then_inc(avg, 1)

    @block.scalar
    def _(act):
        nc.scalar.preload_act_table_set(EXP_LN)
        act.wait_ge(cleared, 2)
        for t in range(tiles):
            act.wait_ge(to_act, n_to_act * t + 1)
            nc.scalar.activation(work[:, 4:5], work[:, 3:4], ACT.Ln).then_inc(acted, 1)
            act.wait_ge(acted, n_acted * t + 1)
            nc.scalar.activation(work[:, 5:6], work[:, 4:5], ACT.Exp, scale=-0.5).then_inc(acted, 1)
            if n_ln:
                act.wait_ge(to_act, n_to_act * t + 2)
                nc.scalar.activation(work[:, 4:5], work[:, 3:4], ACT.Ln).then_inc(acted, 1)
                act.wait_ge(acted, n_acted * t + 3)
                nc.scalar.activation(work[:, 5:6], work[:, 4:5], ACT.Exp, scale=-0.5).then_inc(acted, 1)

    @block.vector
    def _(dve):
        done = [0]

        def link(ins):
            done[0] += 1
            ins.then_inc(chain, 1)
            dve.wait_ge(chain, done[0])

        def newton():
            link(nc.vector.tensor_tensor(work[:, 7:8], work[:, 5:6], work[:, 5:6], ALU.mult))
            link(nc.vector.tensor_tensor(work[:, 7:8], work[:, 7:8], work[:, 3:4], ALU.mult))
            link(nc.vector.tensor_scalar(work[:, 7:8], work[:, 7:8], -0.5, 1.5, ALU.mult, ALU.add))
            link(nc.vector.tensor_tensor(work[:, 6:7], work[:, 7:8], work[:, 5:6], ALU.mult))

        for p in range(2):
            nc.vector.memset(padded[:, p, :, :], 0.0).then_inc(cleared, 1)
        dve.wait_ge(cleared, 2)
        if n_ln:
            dve.wait_ge(fixed, 48)
        for t in range(tiles):
            p = t % 2
            dve.wait_ge(loaded[p], per_load * (t // 2 + 1))
            if add is not None:
                link(nc.vector.tensor_tensor(raw[:, p, :], raw[:, p, :], more[:, p, :], ALU.add))
            for k in range(8):
                last = nc.vector.bn_stats(stats[:, k, :], raw[:, p, 512 * k:512 * k + 512])
                if k < 7:
                    last.then_inc(chain, 1)
                    done[0] += 1
            link(last)
            nc.vector.bn_aggr(mv[:, :], stats[:, :, :].rearrange("p a b -> p (a b)")).then_inc(to_pe, 1)
            dve.wait_ge(avg, n_avg * t + 1)
            link(nc.vector.tensor_copy(work[:, 9:11], ps[:, 0:2]))
            link(nc.vector.tensor_tensor(work[:, 0:1], mv[:, 0:1], work[:, 9:10], ALU.subtract))
            nc.vector.tensor_tensor(work[:, 1:2], work[:, 0:1], work[:, 0:1], ALU.mult).then_inc(to_pe, 1)
            dve.wait_ge(avg, n_avg * t + 2)
            link(nc.vector.tensor_tensor(work[:, 2:3], ps[:, 0:1], work[:, 10:11], ALU.add))
            nc.vector.tensor_scalar(work[:, 3:4], work[:, 2:3], GN_EPS, None, ALU.add).then_inc(to_act, 1)
            dve.wait_ge(acted, n_acted * t + 2)
            newton()
            if t >= 2:
                dve.wait_ge(stored[p], 16 * (16 if n_ln else 8) * (t // 2))
            last = nc.vector.tensor_scalar(
                padded[:, p, 1:IMG + 1, 1:IMG + 1], raw[:, p, :].rearrange("p (a b) -> p a b", b=IMG),
                work[:, 9:10], work[:, 6:7], ALU.subtract, ALU.mult)
            if not n_ln:
                last.then_inc(images, 1)
                continue
            link(last)
            inner = padded[:, p, 1:IMG + 1, 1:IMG + 1]
            w3 = weighted[:, :].rearrange("p (a b) -> p a b", b=IMG)
            c3 = count[:, :].rearrange("p (a b) -> p a b", b=IMG)
            link(nc.vector.tensor_tensor(w3, inner, c3, ALU.mult))
            link(nc.vector.tensor_reduce(mom[:, 0:1], weighted[:, :], AX_X, ALU.add))
            link(nc.vector.tensor_tensor(w3, w3, inner, ALU.mult))
            nc.vector.tensor_reduce(mom[:, 1:2], weighted[:, :], AX_X, ALU.add).then_inc(to_pe, 1)
            dve.wait_ge(avg, n_avg * t + 3)
            link(nc.vector.tensor_copy(work[:, 9:11], ps[:, 0:2]))
            link(nc.vector.tensor_tensor(work[:, 0:1], work[:, 9:10], work[:, 9:10], ALU.mult))
            link(nc.vector.tensor_tensor(work[:, 2:3], work[:, 10:11], work[:, 0:1], ALU.subtract))
            nc.vector.tensor_scalar(work[:, 3:4], work[:, 2:3], LN_EPS, None, ALU.add).then_inc(to_act, 1)
            dve.wait_ge(acted, n_acted * t + 4)
            newton()
            nc.vector.tensor_scalar(
                ln_pad[:, p, :], padded[:, p, :, :].rearrange("p a b -> p (a b)"),
                work[:, 9:10], work[:, 6:7], ALU.subtract, ALU.mult).then_inc(images, 1)


SLOTS = 4 * LANES


def lights(slot, parts, kinds=("squash", "softmax")):
    found = []
    for part in parts:
        for lane in range(LANES):
            starts = [("softmax", r, 8 * r + lane + 1) for r in (0, 1)]
            starts += [("squash", q, 8 * q - 4 + lane + 1) for q in (1, 2)]
            starts.append(("squash", 0, lane - 3))
            for kind, r, at in starts:
                ahead, where = divmod(at + "ABC".index(part), SLOTS)
                if where == slot and kind in kinds:
                    found.append((-ahead, kind, r, lane, part))
    return found


class Pass:

    def __init__(self, n, h, m):
        self.n, self.h, self.m = n, h, m

    def to(self, d):
        if d == 0:
            return self
        if d == 1:
            return Pass(self.n + 1, 1 - self.h, self.m + self.h)
        return Pass(self.n - 1, 1 - self.h, self.m - (1 - self.h))


def run_slots(engine, passes, slot, tail):
    for s in range(SLOTS - 3, SLOTS):
        slot(Pass(-1, 1, -1), s, heavy=False, which=(1,))
    for s in range(SLOTS):
        slot(Pass(0, 0, 0), s, heavy=True, which=(0, 1))
    if passes > 2:
        with engine.Fori(0, passes // 2 - 1) as i:
            for s in range(SLOTS):
                slot(Pass(2 * i + 1, 1, i), s, heavy=True, which=(-1, 0, 1))
            for s in range(SLOTS):
                slot(Pass(2 * i + 2, 0, i + 1), s, heavy=True, which=(-1, 0, 1))
    for s in range(SLOTS):
        slot(Pass(passes - 1, 1, passes // 2 - 1), s, heavy=True, which=(-1, 0))
    tail(Pass(passes, 0, passes // 2))
    for s in range(3):
        slot(Pass(passes, 0, passes // 2), s, heavy=False, which=(-1,))


def routing_phase(nc, ctx, sems, halves, routed, w_sum, w_vote, consts):
    passes = halves.shape[0]

    def sb(n, shape, dt=F32):
        return ctx.enter_context(nc.sbuf_tensor(f"r_{n}", shape, dt))

    def sem(n):
        sems.append(nc.alloc_semaphore(f"r_{n}"))
        return sems[-1]

    win = sb("win", [128, 2, HALF_ROWS, PAD])
    ws = sb("ws", [128, TAPS, C])
    wv_f = sb("wv_f", [128, TAPS * 128])
    wv_r = sb("wv_r", [128, TAPS * 128])
    wv_0 = sb("wv_0", [128, TAPS * 128], BF16)
    wv_1 = sb("wv_1", [128, TAPS * 128], BF16)
    wv_12 = sb("wv_12", [128, TAPS * 128], BF16)
    ident = sb("ident", [128, 128])
    ident_b = sb("ident_b", [128, 128], BF16)
    pick = sb("pick", [128, 2, C])
    eps = sb("eps", [128, 1])
    prod = sb("prod", [128, TAPS, CHUNK])
    temp = sb("temp", [128, len(POOLED), CHUNK])
    sums = sb("sums", [128, 2, 2, CHUNK])
    logit = sb("logit", [128, 2, CHUNK])
    logit9 = sb("logit9", [16, 2, CHUNK])
    cap = sb("cap", [128, 2, LANES, BLK * C])
    sq = sb("sq", [128, 2, LANES, BLK * C])
    norm = sb("norm", [128, 2, LANES, 16])
    lnorm = sb("lnorm", [128, 2, LANES, 16])
    inv = sb("inv", [128, 2, LANES, 16])
    fac = sb("fac", [128, 2, LANES, 16])
    vote = sb("vote", [128, LANES, BLK * C])
    rest = sb("rest", [128, LANES, BLK * C])
    parts = sb("parts", [128, LANES, BLK, 4, C], BF16)
    stack = sb("stack", [128, LANES, CHUNK], BF16)
    top = sb("top", [128, LANES, 144])
    low = sb("low", [128, LANES, 576])
    ex = sb("ex", [128, LANES, 576])
    spread = sb("spread", [128, LANES, 576, CLEN])
    z = sb("z", [128, LANES, 144])
    lz = sb("lz", [128, LANES, 144])
    out_t = sb("out_t", [C, LANES, CHUNK])

    pg = [ctx.enter_context(nc.psum_tensor(f"r_pg{i}", [128, CHUNK], F32)) for i in range(RINGS)]
    pl = ctx.enter_context(nc.psum_tensor("r_pl", [128, CHUNK], F32))
    pl9 = ctx.enter_context(nc.psum_tensor("r_pl9", [128, CHUNK], F32))
    ps = ctx.enter_context(nc.psum_tensor("r_ps", [128, CHUNK], F32))
    pt = ctx.enter_context(nc.psum_tensor("r_pt", [128, CHUNK], F32))
    pt_b = pt[:, :].bitcast(BF16)

    n_dve = TAPS - len(POOLED)
    dve_rank = {g: k for k, g in enumerate(g for g in ORDER if g not in POOLED)}
    pool_rank = {g: k for k, g in enumerate(g for g in ORDER if g in POOLED)}
    batch_of = {g: b for b, gs in enumerate(BATCHES) for g in gs}

    fixed = sem("fixed")
    chain = sem("chain")
    prepared = sem("prepared")
    loaded = [Signal(sem(f"loaded{h}"), 64) for h in range(2)]
    made = Signal(sem("made"), TAPS * SLOTS)
    products = Signal(sem("products"), n_dve * SLOTS, 2)
    copied = Signal(sem("copied"), len(POOLED) * SLOTS, 1)
    pooled = Signal(sem("pooled"), len(POOLED) * SLOTS, 2)
    reduced = Signal(sem("reduced"), 3 * SLOTS, 1)
    stored = Signal(sem("stored"), 16, 1)

    def rounds(name, n, primed=0):
        return [Signal(sem(f"{name}{q}"), LANES, primed) for q in range(n)]

    first_sum = Signal(sem("first_sum"), LANES)
    sum_copied = rounds("sum_copied", 3, 1)
    sum_turned = rounds("sum_turned", 3)
    summed = rounds("summed", 3, 1)
    squared = rounds("squared", 3)
    normed = rounds("normed", 3)
    plus1 = rounds("plus1", 3)
    recip = rounds("recip", 3)
    ratio = rounds("ratio", 3)
    lnormed = rounds("lnormed", 3)
    inverted = rounds("inverted", 3)
    factor = rounds("factor", 3)
    squashed = rounds("squashed", 3)
    voted = rounds("voted", 2)
    part0 = rounds("part0", 2)
    rest1 = rounds("rest1", 2)
    part1 = rounds("part1", 2)
    part2 = rounds("part2", 2)
    parts_turned = rounds("parts_turned", 2)
    stacked = rounds("stacked", 2, 1)
    out_turned = Signal(sem("out_turned"), LANES)
    out_copied = Signal(sem("out_copied"), LANES, 1)
    logit_copied = rounds("logit_copied", 2, 1)
    logit9_copied = rounds("logit9_copied", 2)
    logit_turned = rounds("logit_turned", 2)
    maxed = [Signal(sem(f"maxed{r}"), 2 * LANES) for r in range(2)]
    shifted = rounds("shifted", 2, 1)
    exped = rounds("exped", 2)
    z_ready = rounds("z_ready", 2)
    lz_ready = rounds("lz_ready", 2)
    log_prob = rounds("log_prob", 2)
    prob = rounds("prob", 2)

    turns = []
    for s in range(SLOTS):
        for x in lights(s, "C", ("squash",)) + lights(s, "A"):
            d, kind, r, lane, part = x
            if kind == "softmax":
                turns.append((x, shifted[r], lane + 1))
            elif part == "A":
                turns.append((x, summed[r], lane + 1))
            else:
                turns.append((x, stacked[r] if r < 2 else out_copied, lane + 1))

    def reader_before(x, which):
        at = [u[0] for u in turns].index(x)
        for (d, *_), free, k in reversed(turns[:at]):
            if d in which:
                return free, k + d * free.per
        earlier = {(1,): (), (0, 1): (1,), (-1,): (0,)}.get(which, (0, 1))
        for (d, *_), free, k in reversed(turns):
            if d in earlier:
                return free, k + (d - 1) * free.per
        return None

    def tap_ap(h, lane, tap):
        i, j = divmod(tap, 3)
        return win[:, h, lane * CROWS + i:lane * CROWS + i + CROWS, j:j + IMG]

    def by_capsule(ap):
        return ap.rearrange("p (k o f) -> p k f o", o=CAPS, f=CAPS)

    def over_capsules(ap, k):
        return ap.rearrange("p (k f) -> p k f", f=CAPS).unsqueeze(2).to_broadcast([128, k, CAPS, CAPS])

    block = ctx.enter_context(nc.Block())

    @block.sync
    def _(sp):
        for to, src in ((ws[:, :, :], w_sum), (ident[:, :], consts["ident"]), (pick[:, :, :], consts["pick"])):
            sp.dma_start(to, src).then_inc(fixed, 16)
        for k in range(4):
            sp.dma_start(wv_f[C * k:C * k + C, :], w_vote).then_inc(fixed, 16)
        with sp.Fori(0, passes // 2) as i:
            for h in range(2):
                n = 2 * i + h
                sp.wait_ge(products.sem, products.at(n, -n_dve * SLOTS))
                sp.wait_ge(pooled.sem, pooled.at(n, -len(POOLED) * SLOTS))
                for k in range(CAPS):
                    to = win[C * k:C * k + C, h, :, :].rearrange("p a b -> p (a b)")
                    sp.dma_start(to, halves[n, :, :]).then_inc(loaded[h].sem, 16)

    @block.gpsimd
    def _(pool):
        pool.sem_inc(pooled.sem, pooled.base)

        def slot(p, s, heavy, which):
            if heavy:
                for g in sorted(POOLED, key=ORDER.index):
                    rank = pool_rank[g]
                    k = len(POOLED) * s + rank + 1
                    pool.wait_ge(copied.sem, copied.at(p.n, k))
                    pool.wait_ge(reduced.sem, reduced.at(p.n, 3 * (s - 1) + batch_of[g] + 1))
                    nc.gpsimd.tensor_tensor(
                        prod[:, g, :].rearrange("p (a b) -> p a b", b=IMG),
                        temp[:, rank, :].rearrange("p (a b) -> p a b", b=IMG),
                        tap_ap(p.h, s % LANES, g), ALU.mult).then_inc(pooled.sem, 1)
            for d, kind, r, lane, part in lights(s, "B"):
                if d not in which:
                    continue
                n = p.to(d).n
                if kind == "softmax":
                    pool.wait_ge(lz_ready[r].sem, lz_ready[r].at(n, lane + 1))
                    lo = low[:, lane, :].rearrange("p (k o f) -> p k o f", o=CAPS, f=CAPS)
                    nc.gpsimd.tensor_tensor(lo, lo, over_capsules(lz[:, lane, :], 36),
                                            ALU.subtract).then_inc(log_prob[r].sem, 1)
                elif r < 2:
                    v = vote[:, lane, :].rearrange("p (b c) -> p b c", c=C)
                    left = rest[:, lane, :].rearrange("p (b c) -> p b c", c=C)
                    pool.wait_ge(part0[r].sem, part0[r].at(n, lane + 1))
                    nc.gpsimd.tensor_tensor(left, v, parts[:, lane, :, 0, :], ALU.subtract).then_inc(rest1[r].sem, 1)
                    pool.wait_ge(part1[r].sem, part1[r].at(n, lane + 1))
                    nc.gpsimd.tensor_tensor(parts[:, lane, :, 2, :], left, parts[:, lane, :, 1, :],
                                            ALU.subtract).then_inc(part2[r].sem, 1)

        run_slots(pool, passes, slot, lambda p: None)

    @block.tensor
    def _(pe):
        pe.sem_inc(reduced.sem, reduced.base)
        pe.wait_ge(fixed, 16 * 7)
        pe.wait_ge(prepared, 1)

        def make(n, s, pos):
            tap = ORDER[pos]
            r, lane = s // 8, s % LANES
            use = TAPS * s + pos
            before_s, before_pos = divmod(use - RINGS, TAPS)
            bg = ORDER[before_pos]
            if bg in POOLED:
                pe.wait_ge(copied.sem, copied.at(n, len(POOLED) * before_s + pool_rank[bg] + 1))
            else:
                pe.wait_ge(products.sem, products.at(n, n_dve * before_s + dve_rank[bg] + 1))
            bank = pg[use % RINGS]
            voting = s % 8 < LANES
            if pos == 0:
                ready = stacked[r] if voting else prob[r]
                pe.wait_ge(ready.sem, ready.at(n, lane + 1))
            if voting:
                w = slice(128 * tap, 128 * tap + 128)
                pe.matmul(bank[:, :], wv_0[0:96, w], stack[0:96, lane, :], start=True, stop=False)
                last = pe.matmul(bank[:, :], wv_12[:, w], stack[:, lane, :], start=False, stop=True)
            else:
                for b in range(BLK):
                    kk = 8 * b + 2 * (tap % 4) + tap // 4 if tap < 8 else 32 + b
                    last = pe.transpose(bank[:, 128 * b:128 * b + 128],
                                        spread[:, lane, 16 * kk:16 * kk + 16, :].rearrange("p a b -> p (a b)"),
                                        ident[:, :])
            last.then_inc(made.sem, 1)

        def batch(n, s, b):
            voting = s % 8 < LANES
            r, lane = s // 8, s % LANES
            for signal, rank, per in ((pooled, pool_rank, len(POOLED)), (products, dve_rank, n_dve)):
                own = [rank[tap] for tap in BATCHES[b] if tap in rank]
                if own:
                    pe.wait_ge(signal.sem, signal.at(n, per * s + max(own) + 1))
            k = LANES * r + lane - 1
            if voting and 0 in BATCHES[b]:
                free = logit_copied[k // LANES]
                pe.wait_ge(free.sem, free.at(n, k % LANES + 1) if k >= 0 else free.before(n, LANES))
            if voting and 8 in BATCHES[b]:
                free = shifted[k // LANES] if k >= 0 else sum_copied[0]
                pe.wait_ge(free.sem, free.at(n, k % LANES + 1))
            if not voting and b == 0:
                free = sum_copied[1 + k // LANES] if k >= 0 else sum_copied[2]
                pe.wait_ge(free.sem, free.at(n, k % LANES + 1) if k >= 0 else free.before(n, LANES))
            for tap in BATCHES[b]:
                q = 32 * (tap % 4)
                rhs = prod[:, tap, :]
                if not voting:
                    last = pe.matmul(ps[q:q + 32, :], ws[:, tap, :], rhs, start=tap < 4,
                                     stop=tap in (4, 5, 6, 7), tile_position=(0, q))
                elif tap < 8:
                    last = pe.matmul(pl[q:q + 32, :], pick[:, tap // 4, :], rhs, start=tap < 4,
                                     stop=tap >= 4, tile_position=(0, q))
                else:
                    last = pe.matmul(pl9[0:16, :], pick[:, 0, 0:16], rhs, start=True, stop=True)
            last.then_inc(reduced.sem, 1)

        def sum_uniform(p, x):
            d, kind, r, lane, part = x
            n = p.to(d).n
            if kind == "squash" and r == 0:
                own = p.to(d)
                free = shifted[1] if lane == 0 else sum_copied[0]
                pe.wait_ge(free.sem, free.before(n, LANES) if lane == 0 else free.at(n, lane))
                if lane == 0:
                    pe.wait_ge(loaded[own.h].sem, loaded[own.h].at(own.m, loaded[own.h].per))
                for tap in range(TAPS):
                    q = 32 * (tap % 4)
                    last = pe.matmul(pl9[q:q + 32, :].rearrange("p (a b) -> p a b", b=IMG), ws[:, tap, :],
                                     tap_ap(own.h, lane, tap), start=tap < 4,
                                     stop=tap == 8 or tap in (5, 6, 7), tile_position=(0, q))
                last.then_inc(first_sum.sem, 1)

        def light(p, x, which):
            d, kind, r, lane, part = x
            n = p.to(d).n
            before = reader_before(x, which)
            if before:
                free, k = before
                pe.wait_ge(free.sem, free.at(p.n, k))
            if kind == "squash" and part == "A":
                own = sums[:, int(r > 0), lane % 2, :]
                pe.wait_ge(sum_copied[r].sem, sum_copied[r].at(n, lane + 1))
                for b in range(BLK):
                    last = pe.transpose(pt[:, 128 * b:128 * b + 128], own[:, 128 * b:128 * b + 128], ident[:, :])
                last.then_inc(sum_turned[r].sem, 1)
            elif kind == "squash" and r < 2:
                pe.wait_ge(part2[r].sem, part2[r].at(n, lane + 1))
                for b in range(BLK):
                    last = pe.transpose(pt_b[:, 128 * b:128 * b + 128],
                                        parts[:, lane, b, :, :].rearrange("p a b -> p (a b)"), ident_b[:, :])
                last.then_inc(parts_turned[r].sem, 1)
            elif kind == "squash":
                pe.wait_ge(squashed[2].sem, squashed[2].at(n, lane + 1))
                for b in range(BLK):
                    last = pe.transpose(pt[0:C, 128 * b:128 * b + 128], sq[:, 1, lane, C * b:C * b + C], ident[:, :])
                last.then_inc(out_turned.sem, 1)
            else:
                pe.wait_ge(logit_copied[r].sem, logit_copied[r].at(n, lane + 1))
                pe.wait_ge(logit9_copied[r].sem, logit9_copied[r].at(n, lane + 1))
                for b in range(BLK):
                    pe.transpose(pt[:, 128 * b:128 * b + 128], logit[:, lane % 2, 128 * b:128 * b + 128], ident[:, :])
                for b in range(BLK):
                    last = pe.transpose(pl9[:, 16 * b:16 * b + 16], logit9[:, lane % 2, 128 * b:128 * b + 128],
                                        ident[0:16, 0:16])
                last.then_inc(logit_turned[r].sem, 1)

        def slot(p, s, heavy, which):
            back = [x for x in lights(s, "C", ("squash",)) if x[0] in which]
            front = [x for x in lights(s, "A") if x[0] in which]
            for pos in range(3):
                if heavy:
                    make(p.n, s, pos)
            for x in back[:1]:
                light(p, x, which)
            if heavy and (s > 0 or -1 in which):
                behind = p if s > 0 else p.to(-1)
                batch(behind.n, (s - 1) % SLOTS, 1)
                batch(behind.n, (s - 1) % SLOTS, 2)
            for x in back[1:]:
                light(p, x, which)
            for pos in range(3, 7):
                if heavy:
                    make(p.n, s, pos)
            for x in front:
                sum_uniform(p, x)
            for x in front[:1]:
                light(p, x, which)
            for pos in range(7, 9):
                if heavy:
                    make(p.n, s, pos)
            for x in front[1:]:
                light(p, x, which)
            if heavy:
                batch(p.n, s, 0)

        def tail(p):
            batch(p.to(-1).n, SLOTS - 1, 1)
            batch(p.to(-1).n, SLOTS - 1, 2)

        run_slots(pe, passes, slot, tail)

    @block.scalar
    def _(act):
        for sig in (copied, *sum_copied, *stacked, out_copied, *logit_copied, stored):
            act.sem_inc(sig.sem, sig.base)
        nc.scalar.preload_act_table_set(EXP_LN)
        act.wait_ge(prepared, 1)

        def evacuate(n, kind, r, lane):
            if kind == "squash" and r == 0:
                act.wait_ge(first_sum.sem, first_sum.at(n, lane + 1))
                nc.scalar.mul(sums[:, 0, lane % 2, :], pl9[:, :], 1.0 / CAPS).then_inc(sum_copied[0].sem, 1)
            elif kind == "squash":
                act.wait_ge(reduced.sem, reduced.at(n, 3 * (8 * r - 4 + lane) + 3))
                nc.scalar.copy(sums[:, 1, lane % 2, :], ps[:, :]).then_inc(sum_copied[r].sem, 1)
            else:
                act.wait_ge(reduced.sem, reduced.at(n, 3 * (8 * r + lane) + 3))
                nc.scalar.copy(logit[:, lane % 2, :], pl[:, :]).then_inc(logit_copied[r].sem, 1)
                nc.scalar.copy(logit9[:, lane % 2, :], pl9[0:16, :]).then_inc(logit9_copied[r].sem, 1)

        def first_functions(n, kind, r, lane):
            k = lane + 1
            if kind == "squash":
                own = int(r > 0)
                act.wait_ge(normed[r].sem, normed[r].at(n, k))
                nc.scalar.activation(lnorm[:, own, lane, :], norm[:, own, lane, :], ACT.Ln,
                                     bias=eps[:, 0:1]).then_inc(lnormed[r].sem, 1)
                act.wait_ge(lnormed[r].sem, lnormed[r].at(n, k))
                nc.scalar.activation(inv[:, own, lane, :], lnorm[:, own, lane, :], ACT.Exp,
                                     scale=-0.5).then_inc(inverted[r].sem, 1)
            else:
                act.wait_ge(shifted[r].sem, shifted[r].at(n, k))
                nc.scalar.activation(ex[:, lane, :], low[:, lane, :], ACT.Exp).then_inc(exped[r].sem, 1)

        def second_functions(n, kind, r, lane):
            k = lane + 1
            if kind == "softmax":
                act.wait_ge(z_ready[r].sem, z_ready[r].at(n, k))
                nc.scalar.activation(lz[:, lane, :], z[:, lane, :], ACT.Ln).then_inc(lz_ready[r].sem, 1)
            elif r < 2:
                v = vote[:, lane, :].rearrange("p (b c) -> p b c", c=C)
                act.wait_ge(voted[r].sem, voted[r].at(n, k))
                nc.scalar.copy(parts[:, lane, :, 0, :], v).then_inc(part0[r].sem, 1)
                nc.scalar.copy(parts[:, lane, :, 3, :], v)
                act.wait_ge(rest1[r].sem, rest1[r].at(n, k))
                nc.scalar.copy(parts[:, lane, :, 1, :],
                               rest[:, lane, :].rearrange("p (b c) -> p b c", c=C)).then_inc(part1[r].sem, 1)

        def finish_squash(p, r, lane):
            if r < 2:
                act.wait_ge(parts_turned[r].sem, parts_turned[r].at(p.n, lane + 1))
                nc.scalar.copy(stack[:, lane, :], pt_b[:, 0:CHUNK]).then_inc(stacked[r].sem, 1)
                return
            if lane == 0:
                act.wait_ge(stored.sem, stored.at(p.n, 0))
            act.wait_ge(out_turned.sem, out_turned.at(p.n, lane + 1))
            nc.scalar.copy(out_t[:, lane, :], pt[0:C, :]).then_inc(out_copied.sem, 1)
            if lane == LANES - 1:
                act.wait_ge(out_copied.sem, out_copied.at(p.n, LANES))
                act.dma_start(routed[p.n, :, :], out_t[:, :, :].rearrange("p l x -> p (l x)")).then_inc(stored.sem, 16)

        def slot(p, s, heavy, which):
            back = [x for x in lights(s, "C", ("squash",)) if x[0] in which]
            for d, kind, r, lane, part in back[:1]:
                finish_squash(p.to(d), r, lane)
            if heavy:
                for g in sorted(POOLED, key=ORDER.index):
                    pos = ORDER.index(g)
                    act.wait_ge(made.sem, made.at(p.n, TAPS * s + pos + 1))
                    act.wait_ge(pooled.sem, pooled.at(p.n, len(POOLED) * (s - 1) + pool_rank[g] + 1))
                    nc.scalar.copy(temp[:, pool_rank[g], :], pg[(TAPS * s + pos) % RINGS][:, :]).then_inc(copied.sem, 1)
            for d, kind, r, lane, part in lights(s, "A"):
                if d in which and not (kind == "squash" and r == 0):
                    evacuate(p.to(d).n, kind, r, lane)
            for d, kind, r, lane, part in back[1:]:
                finish_squash(p.to(d), r, lane)
            for d, kind, r, lane, part in lights(s, "A", ("squash",)):
                if d in which and r == 0:
                    evacuate(p.to(d).n, kind, r, lane)
            for d, kind, r, lane, part in lights(s, "C", ("softmax",)):
                if d in which:
                    n = p.to(d).n
                    act.wait_ge(log_prob[r].sem, log_prob[r].at(n, lane + 1))
                    nc.scalar.activation(spread[:, lane, :, :],
                                         low[:, lane, :].unsqueeze(2).to_broadcast([128, 576, CLEN]),
                                         ACT.Exp).then_inc(prob[r].sem, 1)
            for d, kind, r, lane, part in lights(s, "B"):
                if d in which:
                    second_functions(p.to(d).n, kind, r, lane)
            for d, kind, r, lane, part in lights(s, "A"):
                if d in which:
                    first_functions(p.to(d).n, kind, r, lane)

        run_slots(act, passes, slot, lambda p: None)
        act.wait_ge(stored.sem, stored.at(passes, 0))

    @block.vector
    def _(dve):
        for sig in (products, *summed, *shifted):
            dve.sem_inc(sig.sem, sig.base)
        step = [0]

        def link(ins):
            step[0] += 1
            ins.then_inc(chain, 1)
            dve.wait_ge(chain, step[0])

        dve.wait_ge(fixed, 16 * 7)
        link(nc.vector.tensor_copy(wv_0[:, :], wv_f[:, :]))
        link(nc.vector.tensor_tensor(wv_r[:, :], wv_f[:, :], wv_0[:, :], ALU.subtract))
        link(nc.vector.tensor_copy(wv_1[:, :], wv_r[:, :]))
        link(nc.vector.tensor_copy(wv_12[0:64, :], wv_1[0:64, :]))
        link(nc.vector.memset(wv_12[64:96, :], 0.0))
        link(nc.vector.tensor_tensor(wv_12[96:128, :], wv_r[96:128, :], wv_1[96:128, :], ALU.subtract))
        link(nc.vector.memset(eps[:, :], SQUASH_EPS))
        nc.vector.tensor_copy(ident_b[:, :], ident[:, :]).then_inc(prepared, 1)

        def product(p, s, g):
            use = TAPS * s + ORDER.index(g)
            dve.wait_ge(made.sem, made.at(p.n, use + 1))
            dve.wait_ge(reduced.sem, reduced.at(p.n, 3 * (s - 1) + batch_of[g] + 1))
            nc.vector.tensor_tensor(
                prod[:, g, :].rearrange("p (a b) -> p a b", b=IMG),
                pg[use % RINGS][:, :].rearrange("p (a b) -> p a b", b=IMG),
                tap_ap(p.h, s % LANES, g), ALU.mult).then_inc(products.sem, 1)

        def light_a(n, kind, r, lane):
            k = lane + 1
            if kind == "squash":
                own = int(r > 0)
                c, s2, nm, fc = cap[:, own, lane, :], sq[:, own, lane, :], norm[:, own, lane, :], fac[:, own, lane, :]
                dve.wait_ge(sum_turned[r].sem, sum_turned[r].at(n, k))
                nc.vector.tensor_reduce(c, pt[:, :].rearrange("p (b g c) -> p b c g", b=BLK, c=C),
                                        AX_X, ALU.add).then_inc(summed[r].sem, 1)
                dve.wait_ge(summed[r].sem, summed[r].at(n, k))
                nc.vector.tensor_tensor(s2, c, c, ALU.mult).then_inc(squared[r].sem, 1)
                dve.wait_ge(squared[r].sem, squared[r].at(n, k))
                nc.vector.tensor_reduce(nm, s2.rearrange("p (k u) -> p k u", u=CLEN), AX_X, ALU.add).then_inc(normed[r].sem, 1)
                dve.wait_ge(normed[r].sem, normed[r].at(n, k))
                nc.vector.tensor_scalar(fc, nm, 1.0, None, ALU.add).then_inc(plus1[r].sem, 1)
                dve.wait_ge(plus1[r].sem, plus1[r].at(n, k))
                nc.vector.reciprocal(fc, fc).then_inc(recip[r].sem, 1)
                dve.wait_ge(recip[r].sem, recip[r].at(n, k))
                nc.vector.tensor_tensor(fc, fc, nm, ALU.mult).then_inc(ratio[r].sem, 1)
                return
            dve.wait_ge(logit_turned[r].sem, logit_turned[r].at(n, k))
            pieces = ((pt[:, :], 0, 32), (pl9[:, 0:64], 32, 36))
            for src, a, b in pieces:
                nc.vector.tensor_reduce(top[:, lane, 4 * a:4 * b].rearrange("p (k f) -> p k f", f=CAPS),
                                        by_capsule(src), AX_X, ALU.max).then_inc(maxed[r].sem, 1)
            dve.wait_ge(maxed[r].sem, maxed[r].at(n, 2 * k))
            for src, a, b in pieces:
                last = nc.vector.tensor_tensor(
                    low[:, lane, 16 * a:16 * b].rearrange("p (k o f) -> p k o f", o=CAPS, f=CAPS),
                    src.rearrange("p (k o f) -> p k o f", o=CAPS, f=CAPS),
                    over_capsules(top[:, lane, 4 * a:4 * b], b - a), ALU.subtract)
            last.then_inc(shifted[r].sem, 1)

        def light_b(n, kind, r, lane):
            k = lane + 1
            if kind == "softmax":
                dve.wait_ge(exped[r].sem, exped[r].at(n, k))
                nc.vector.tensor_reduce(z[:, lane, :].rearrange("p (k f) -> p k f", f=CAPS),
                                        by_capsule(ex[:, lane, :]), AX_X, ALU.add).then_inc(z_ready[r].sem, 1)
                return
            own = int(r > 0)
            fc = fac[:, own, lane, :]
            dve.wait_ge(ratio[r].sem, ratio[r].at(n, k))
            dve.wait_ge(inverted[r].sem, inverted[r].at(n, k))
            nc.vector.tensor_tensor(fc, fc, inv[:, own, lane, :], ALU.mult).then_inc(factor[r].sem, 1)
            dve.wait_ge(factor[r].sem, factor[r].at(n, k))
            f = fc.unsqueeze(2).to_broadcast([128, 16, CLEN])
            c = cap[:, own, lane, :].rearrange("p (k u) -> p k u", u=CLEN)
            to = (vote[:, lane, :] if r == 0 else sq[:, 1, lane, :]).rearrange("p (k u) -> p k u", u=CLEN)
            last = nc.vector.tensor_tensor(to, c, f, ALU.mult)
            if r == 0:
                last.then_inc(voted[0].sem, 1)
                return
            last.then_inc(squashed[r].sem, 1)
            if r == 1:
                dve.wait_ge(squashed[1].sem, squashed[1].at(n, k))
                nc.vector.tensor_tensor(vote[:, lane, :], vote[:, lane, :], sq[:, 1, lane, :], ALU.add).then_inc(voted[1].sem, 1)

        def slot(p, s, heavy, which):
            own = [g for g in ORDER if g not in POOLED] if heavy else []
            for g in own[:1]:
                product(p, s, g)
            for d, kind, r, lane, part in lights(s, "B"):
                if d in which:
                    light_b(p.to(d).n, kind, r, lane)
            for g in own[1:5]:
                product(p, s, g)
            front = [x for x in lights(s, "A") if x[0] in which]
            for d, kind, r, lane, part in front[:1]:
                light_a(p.to(d).n, kind, r, lane)
            for g in own[5:]:
                product(p, s, g)
            for d, kind, r, lane, part in front[1:]:
                light_a(p.to(d).n, kind, r, lane)

        run_slots(dve, passes, slot, lambda p: None)


UROWS = 16
UNIT = UROWS * IMG
QB = UNIT // CHUNK
KB = UNIT // 128
QUAD = 4
QUADS = HEADS // QUAD
STEPS = QUADS * QB * KB
TILES = [(0, 6), (6, 12), (12, 16)]
SIX = [(0, 0), (0, 1), (0, 2), (1, 0), (1, 1), (2, 0)]
KROWS = len(SIX) * HD
NPART = 3

TASKS = {0: (0, "max", 1), 1: (-1, "turn", 3), 2: (-1, "back", 3),
         3: (-1, "out", 3), 4: (-1, "out", 4), 5: (-1, "out", 5),
         6: (2, "qk", 0), 7: (2, "qk", 1), 8: (2, "qk", 2), 9: (0, "turn", 0), 10: (0, "back", 0),
         11: (2, "qk", 3), 12: (2, "qk", 4), 13: (2, "qk", 5), 14: (1, "v", 0), 15: (1, "v", 1),
         16: (1, "v", 2), 17: (0, "turn", 1), 18: (0, "back", 1), 19: (1, "max", 0),
         25: (0, "turn", 2), 26: (0, "back", 2), 27: (0, "out", 0), 28: (0, "out", 1), 29: (0, "out", 2)}


def run_units(engine, units, unit):
    for n, which in ((-2, (2,)), (-1, (1, 2)), (0, (0, 1, 2)), (1, (-1, 0, 1, 2))):
        unit(Pass(n, n % 2, n // 2), which)
    if units > 4:
        with engine.Fori(0, units // 2 - 2) as i:
            unit(Pass(2 * i + 2, 0, i + 1), (-1, 0, 1, 2))
            unit(Pass(2 * i + 3, 1, i + 1), (-1, 0, 1, 2))
    for n, which in ((units - 2, (-1, 0, 1)), (units - 1, (-1, 0)), (units, (-1,))):
        unit(Pass(n, n % 2, n // 2), which)


def offset(p, d):
    for _ in range(abs(d)):
        p = p.to(1 if d > 0 else -1)
    return p


def attention_phase(nc, ctx, sems, halves, ln_halves, mixed, moments, w_r, w_qkv, w_p, consts):
    units = halves.shape[0] * 2
    R = 3 * C
    scale = float(HD) ** -0.5
    spare = nc.dram_tensor("qk_parts", [2, NPART, 2 * C2, UNIT], BF16, kind="Internal").ap()
    max_rows = nc.dram_tensor("max_rows", [2, QUADS, NPART * QUAD * KB, 128], BF16, kind="Internal").ap()

    def sb(n, shape, dt=F32):
        return ctx.enter_context(nc.sbuf_tensor(f"a_{n}", shape, dt))

    def sem(n):
        sems.append(nc.alloc_semaphore(f"a_{n}"))
        return sems[-1]

    zw = sb("zw", [R, 2, (UROWS + 2) * IMG])
    tw = sb("tw", [R, 2, (UROWS + 2) * IMG])
    wr_a = sb("wr_a", [128, 3, R])
    wr_b = sb("wr_b", [C2 - 128, 3, R])
    wq_a = sb("wq_a", [128, 3 * C2])
    wq_b = sb("wq_b", [C2 - 128, 3 * C2])
    wc = sb("wc", [R, 3, 3 * C2])
    wp = sb("wp", [128, QUADS, 3, R])
    ident = sb("ident", [128, 128])
    ident_b = sb("ident_b", [128, 128], BF16)
    pieces = sb("pieces", [6 * HD, len(TILES), NPART, UNIT], BF16)
    left = sb("left", [6 * HD, 2, CHUNK])
    qs = sb("qs", [128, 2, HEADS, UNIT], BF16)
    ks = sb("ks", [128, 2, HEADS, UNIT], BF16)
    va = sb("va", [128, 2, KB, HEADS, 32])
    big = sb("big", [128, 2, HEADS * KB])
    top = sb("top", [128, QUAD * KB])
    mleft = sb("mleft", [128, 2, QUAD * KB])
    mparts = sb("mparts", [128, NPART, QUAD * KB], BF16)
    mrow = sb("mrow", [NPART * QUAD * KB, 128], BF16)
    RING = 2 * QUAD
    ex = sb("ex", [128, RING, CHUNK])
    oc = sb("oc", [128, CHUNK])
    rz = sb("rz", [128, BLK * QUAD])
    rb = sb("rb", [128, BLK, QUAD, 32])
    on = sb("on", [128, QUADS * QB, CHUNK])
    t1 = sb("t1", [R, 3, CHUNK])
    sqr = sb("sqr", [R, CHUNK])
    mo = sb("mo", [R, 2, 12])

    sc = [ctx.enter_context(nc.psum_tensor(f"a_sc{i}", [128, CHUNK], F32)) for i in range(QUAD)]
    mp = [ctx.enter_context(nc.psum_tensor(f"a_mp{i}", [128, CHUNK], F32)) for i in range(2)]
    po = ctx.enter_context(nc.psum_tensor("a_po", [128, CHUNK], F32))
    pm = ctx.enter_context(nc.psum_tensor("a_pm", [128, CHUNK], F32))
    pm_b = pm[:, :].bitcast(BF16)

    fixed = sem("fixed")
    chain = sem("chain")
    combined = sem("combined")
    wc_copied = sem("wc_copied")
    prepared = sem("prepared")
    zw_in = [Signal(sem(f"zw_in{h}"), 48) for h in range(2)]
    tw_in = [Signal(sem(f"tw_in{h}"), 48) for h in range(2)]
    qk_made = Signal(sem("qk_made"), 6)
    lead = Signal(sem("lead"), 6)
    remain = Signal(sem("remain"), 6)
    second = Signal(sem("second"), 6)
    third = Signal(sem("third"), 6)
    spared = Signal(sem("spared"), 48, 1)
    stack_in = [Signal(sem(f"stack_in{q}"), 16 * 12) for q in range(QUADS)]
    v_made = Signal(sem("v_made"), 3)
    v_done = Signal(sem("v_done"), 3)
    max_made = Signal(sem("max_made"), 2 * HEADS * KB)
    maxed = Signal(sem("maxed"), 2 * HEADS * KB, 2)
    m0 = Signal(sem("m0"), 2)
    m1 = Signal(sem("m1"), 2)
    m2 = Signal(sem("m2"), 2)
    m3 = Signal(sem("m3"), 2)
    negated = Signal(sem("negated"), 2)
    neg_turned = Signal(sem("neg_turned"), 2)
    neg_copied = Signal(sem("neg_copied"), 2)
    neg_spared = Signal(sem("neg_spared"), 32, 1)
    neg_in = [Signal(sem(f"neg_in{q}"), 16) for q in range(QUADS)]
    score_made = Signal(sem("score_made"), QUAD * STEPS)
    exped = Signal(sem("exped"), QUAD * STEPS)
    valued = Signal(sem("valued"), STEPS)
    o_copied = Signal(sem("o_copied"), 4)
    o_turned = Signal(sem("o_turned"), 4)
    z_inv = Signal(sem("z_inv"), 4)
    rb_ready = Signal(sem("rb_ready"), 4)
    rb_turned = Signal(sem("rb_turned"), 4)
    o_normed = Signal(sem("o_normed"), 4)
    out_made = Signal(sem("out_made"), 6)
    t1_done = Signal(sem("t1_done"), 6)
    sq_done = Signal(sem("sq_done"), 6)
    t1_stored = [Signal(sem(f"t1_stored{i}"), 32, 1) for i in range(3)]
    mo_stored = [Signal(sem(f"mo_stored{h}"), 16, 1) for h in range(2)]

    readers = {"max": (neg_copied,), "turn": (z_inv,), "back": (o_normed,), "out": (t1_done,),
               "qk": (remain,), "v": (v_done,)}

    def reader_before(t, which):
        for s in range(t - 1, -1, -1):
            if s in TASKS and TASKS[s][0] in which:
                d, kind, k = TASKS[s]
                return readers[kind][0], k + 1 + d * readers[kind][0].per
        earlier = {(2,): (), (1, 2): (2,), (0, 1, 2): (1, 2), (-1, 0): (-1, 0, 1), (-1,): (-1, 0)}.get(which, (-1, 0, 1, 2) if 2 not in which else (0, 1, 2))
        for s in range(STEPS - 1, -1, -1):
            if s in TASKS and TASKS[s][0] in earlier:
                d, kind, k = TASKS[s]
                return readers[kind][0], k + 1 + (d - 1) * readers[kind][0].per
        return None

    block = ctx.enter_context(nc.Block())

    @block.sync
    def _(sp):
        for to, src in ((wr_a[:, :, :], w_r[0:128]), (wr_b[:, :, :], w_r[128:C2]), (wq_a[:, :], w_qkv[0:128, :]),
                        (wq_b[:, :], w_qkv[128:C2, :]), (ident[:, :], consts["ident"])):
            sp.dma_start(to, src).then_inc(fixed, 16)
        for q in range(QUADS):
            sp.dma_start(wp[:, q, :, :], w_p[q]).then_inc(fixed, 16)

        def load_window(to, src, p, arrived):
            image = src[p.m, :, :].rearrange("c (a b) -> c a b", b=PAD)
            for j in range(3):
                sp.dma_start(to[C * j:C * j + C, p.h, :].rearrange("p (a b) -> p a b", b=IMG),
                             image[:, UROWS * p.h:UROWS * p.h + UROWS + 2, j:j + IMG]).then_inc(arrived[p.h].sem, 16)

        def load_stack(p, quad):
            rows = slice(QUAD * HD * quad, QUAD * HD * (quad + 1))
            for k, parts in enumerate(SIX):
                for to, part, first in ((qs, parts[0], 0), (ks, parts[1], C2)):
                    src = spare[p.h, part, first + rows.start:first + rows.stop, :]
                    sp.dma_start(to[HD * k:HD * k + HD, p.h, QUAD * quad:QUAD * quad + QUAD, :],
                                 src.rearrange("(h d) x -> d h x", d=HD)).then_inc(stack_in[quad].sem, 16)

        def load_max(p, quad):
            sp.wait_ge(neg_copied.sem, neg_copied.at(p.n, quad + 1))
            sp.dma_start(max_rows[p.h, quad, :, :], mrow[:, :]).then_inc(neg_spared.sem, 16)
            sp.wait_ge(neg_spared.sem, neg_spared.at(p.n, 16 * (quad + 1)))
            sp.dma_start(qs[KROWS:KROWS + NPART, p.h, QUAD * quad:QUAD * quad + QUAD, :].rearrange("p h x -> p (h x)"),
                         max_rows[p.h, quad, :, :].rearrange("(k a) x -> k (a x)", k=NPART)).then_inc(neg_in[quad].sem, 16)

        def store_mixed(p, qb):
            for i in range(3):
                sp.wait_ge(t1_done.sem, t1_done.at(p.n, 3 * qb + i + 1))
                sp.dma_start(mixed[p.n, i, :, CHUNK * qb:CHUNK * qb + CHUNK], t1[:, i, :]).then_inc(t1_stored[i].sem, 16)
            if qb == QB - 1:
                sp.wait_ge(sq_done.sem, sq_done.at(p.n, 6))
                sp.dma_start(moments[:, p.n, :], mo[:, p.h, :]).then_inc(mo_stored[p.h].sem, 16)

        sp.wait_ge(prepared, 1)

        def unit(p, which):
            if 2 in which:
                if 0 in which:
                    sp.wait_ge(v_made.sem, v_made.at(p.n, 3))
                load_window(zw, ln_halves, offset(p, 2), zw_in)
            if 0 in which:
                load_max(p, 1)
                if -1 in which:
                    sp.wait_ge(t1_done.sem, t1_done.at(p.n, 6 - 2 * t1_done.per) if not isinstance(p.n, int) or p.n >= 2 else t1_done.at(0, 1))
                load_window(tw, halves, p, tw_in)
            if -1 in which:
                store_mixed(p.to(-1), 1)
            if 2 in which:
                a = offset(p, 2)
                sp.wait_ge(third.sem, third.at(a.n, 6))
                for k, (lo, hi) in enumerate(TILES):
                    rows = (hi - lo) * HD
                    sp.dma_start(spare[a.h, :, lo * HD:hi * HD, :].rearrange("r p x -> p r x"),
                                 pieces[0:rows, k, :, :]).then_inc(spared.sem, 16)
                sp.wait_ge(spared.sem, spared.at(a.n, 48))
                if 0 in which:
                    sp.wait_ge(score_made.sem, score_made.at(p.n, QUAD * STEPS // 2))
                load_stack(a, 0)
            if 1 in which:
                load_max(p.to(1), 0)
            if 0 in which:
                store_mixed(p, 0)
            if 2 in which:
                if 0 in which:
                    sp.wait_ge(score_made.sem, score_made.at(p.n, QUAD * STEPS))
                load_stack(offset(p, 2), 1)

        run_units(sp, units, unit)
        for i in range(3):
            sp.wait_ge(t1_stored[i].sem, t1_stored[i].at(units, 0))
        for h in range(2):
            sp.wait_ge(mo_stored[h].sem, mo_stored[h].at(units // 2, 0))

    @block.gpsimd
    def _(pool):
        def unit(p, which):
            for t in sorted(TASKS):
                d, kind, k = TASKS[t]
                if d in which and kind == "qk":
                    n = offset(p, d).n
                    qb, tile = divmod(k, 3)
                    rows = (TILES[tile][1] - TILES[tile][0]) * HD
                    cols = slice(CHUNK * qb, CHUNK * qb + CHUNK)
                    pool.wait_ge(second.sem, second.at(n, k + 1))
                    nc.gpsimd.tensor_tensor(pieces[0:rows, tile, 2, cols], left[0:rows, k % 2, :],
                                            pieces[0:rows, tile, 1, cols], ALU.subtract).then_inc(third.sem, 1)

        run_units(pool, units, unit)

    @block.tensor
    def _(pe):
        pe.wait_ge(fixed, 16 * 7)
        for i in range(3):
            if i:
                pe.wait_ge(wc_copied, i)
            pe.matmul(pm[0:R, 0:3 * C2], wr_a[:, i, :], wq_a[:, :], start=True, stop=False)
            pe.matmul(pm[0:R, 0:3 * C2], wr_b[:, i, :], wq_b[:, :], start=False, stop=True).then_inc(combined, 1)
        pe.wait_ge(wc_copied, 3)
        pe.wait_ge(prepared, 1)

        def task(p, t, which):
            if t not in TASKS or TASKS[t][0] not in which:
                return
            d, kind, k = TASKS[t]
            own = offset(p, d)
            before = reader_before(t, which)
            if before:
                pe.wait_ge(before[0].sem, before[0].at(p.n, before[1]))
            if kind == "qk":
                qb, tile = divmod(k, 3)
                lo, hi = TILES[tile]
                if k == 0:
                    pe.wait_ge(zw_in[own.h].sem, zw_in[own.h].at(own.m, 48))
                for i in range(3):
                    first = (CROWS * qb + i) * IMG
                    last = pe.matmul(pm[0:(hi - lo) * HD, :], wc[:, i, lo * HD:hi * HD],
                                     zw[:, own.h, first:first + CHUNK], start=i == 0, stop=i == 2)
                last.then_inc(qk_made.sem, 1)
            elif kind == "v":
                for b in range(3 * k, min(3 * k + 3, KB)):
                    for i in range(3):
                        first = (2 * b + i) * IMG
                        last = pe.matmul(pm[:, C2 * (b % 3):C2 * (b % 3) + C2], zw[:, own.h, first:first + 128],
                                         wc[:, i, 2 * C2:3 * C2], start=i == 0, stop=i == 2)
                last.then_inc(v_made.sem, 1)
            elif kind == "max":
                pe.wait_ge(negated.sem, negated.at(own.n, k + 1))
                pe.transpose(pm_b[0:96, 0:128], mparts[:, :, :].rearrange("p a b -> p (a b)"),
                             ident_b[:, :]).then_inc(neg_turned.sem, 1)
            elif kind == "turn":
                pe.wait_ge(o_copied.sem, o_copied.at(own.n, k + 1))
                for b in range(BLK):
                    last = pe.transpose(pm[:, 128 * b:128 * b + 128], oc[:, 128 * b:128 * b + 128], ident[:, :])
                last.then_inc(o_turned.sem, 1)
            elif kind == "back":
                pe.wait_ge(rb_ready.sem, rb_ready.at(own.n, k + 1))
                for b in range(BLK):
                    last = pe.transpose(pm[:, 128 * b:128 * b + 128], rb[:, b, :, :].rearrange("p a b -> p (a b)"), ident[:, :])
                last.then_inc(rb_turned.sem, 1)
            elif kind == "out":
                qb, i = divmod(k, 3)
                pe.wait_ge(o_normed.sem, o_normed.at(own.n, QB + qb + 1))
                for quad in range(QUADS):
                    last = pe.matmul(pm[0:R, :], wp[:, quad, i, :], on[:, QB * quad + qb, :],
                                     start=quad == 0, stop=quad == 1)
                last.then_inc(out_made.sem, 1)

        def score(p, t, x):
            quad, qb, kb = t // 16, t // 8 % 2, t % 8
            k = QUAD * t + x
            head = QUAD * quad + x
            if t % 16 == 0 and x == 0:
                pe.wait_ge(neg_in[quad].sem, neg_in[quad].at(p.n, 16))
            if not (isinstance(p.n, int) and p.n == 0 and k < QUAD):
                pe.wait_ge(exped.sem, exped.at(p.n, k - QUAD + 1))
            pe.matmul(sc[x][:, :], ks[0:KROWS + NPART, p.h, head, 128 * kb:128 * kb + 128],
                      qs[0:KROWS + NPART, p.h, head, CHUNK * qb:CHUNK * qb + CHUNK],
                      start=True, stop=True).then_inc(score_made.sem, 1)

        def maximum(p, t, x):
            k = 4 * t + x
            head, q = divmod(k // 2, KB)
            half = x % 2
            if k % (2 * QUAD * KB) == 0:
                pe.wait_ge(stack_in[head // QUAD].sem, stack_in[head // QUAD].at(p.n, 16 * 12))
            pe.wait_ge(maxed.sem, maxed.at(p.n, k - 1))
            pe.matmul(mp[half][:, :], qs[0:KROWS, p.h, head, 128 * q:128 * q + 128],
                      ks[0:KROWS, p.h, head, CHUNK * half:CHUNK * half + CHUNK],
                      start=True, stop=True).then_inc(max_made.sem, 1)

        def values(p, t):
            quad, qb, kb = t // 16, t // 8 % 2, t % 8
            g = t // 8
            pe.wait_ge(exped.sem, exped.at(p.n, QUAD * t + QUAD))
            if t == 0:
                pe.wait_ge(v_done.sem, v_done.at(p.n, 3))
            if kb == 0 and not (isinstance(p.n, int) and p.n == 0 and g == 0):
                pe.wait_ge(o_copied.sem, o_copied.at(p.n, g))
            for x in range(QUAD):
                last = pe.matmul(po[32 * x:32 * x + 32, :], va[:, p.h, kb, QUAD * quad + x, :],
                                 ex[:, (QUAD * t + x) % RING, :], start=kb == 0, stop=kb == KB - 1,
                                 tile_position=(0, 32 * x))
            last.then_inc(valued.sem, 1)

        def unit(p, which):
            for t in range(STEPS):
                for x in range(QUAD):
                    if 0 in which:
                        score(p, t, x)
                    if 1 in which:
                        maximum(p.to(1), t, x)
                    if x == 1 and t == 0 and -1 in which:
                        values(p.to(-1), STEPS - 1)
                    elif x == 1 and t and 0 in which:
                        values(p, t - 1)
                task(p, t, which)

        run_units(pe, units, unit)

    @block.scalar
    def _(act):
        for sig in (*t1_stored, spared, neg_spared, *mo_stored):
            act.sem_inc(sig.sem, sig.base)
        nc.scalar.preload_act_table_set(EXP_LN)
        for i in range(3):
            act.wait_ge(combined, i + 1)
            nc.scalar.copy(wc[:, i, :], pm[0:R, 0:3 * C2]).then_inc(wc_copied, 1)
        act.wait_ge(prepared, 1)

        def task(p, t, which):
            if t not in TASKS or TASKS[t][0] not in which:
                return
            d, kind, k = TASKS[t]
            own = offset(p, d)
            if kind == "qk":
                qb, tile = divmod(k, 3)
                rows = (TILES[tile][1] - TILES[tile][0]) * HD
                cols = slice(CHUNK * qb, CHUNK * qb + CHUNK)
                if k == 0:
                    act.wait_ge(spared.sem, spared.at(own.n, 0))
                act.wait_ge(qk_made.sem, qk_made.at(own.n, k + 1))
                nc.scalar.copy(pieces[0:rows, tile, 0, cols], pm[0:rows, :]).then_inc(lead.sem, 1)
            elif kind == "v":
                nb = min(3, KB - 3 * k)
                act.wait_ge(v_made.sem, v_made.at(own.n, k + 1))
                nc.scalar.copy(va[:, own.h, 3 * k:3 * k + nb, :, 0:HD],
                               pm[:, 0:C2 * nb].rearrange("p (b h d) -> p b h d", h=HEADS, d=HD)).then_inc(v_done.sem, 1)
            elif kind == "max":
                act.wait_ge(neg_turned.sem, neg_turned.at(own.n, k + 1))
                act.wait_ge(neg_spared.sem, neg_spared.at(own.n, 16 * k))
                nc.scalar.copy(mrow[:, :], pm_b[0:96, 0:128]).then_inc(neg_copied.sem, 1)

        def late_task(p, t, which):
            if t not in TASKS or TASKS[t][0] not in which:
                return
            d, kind, k = TASKS[t]
            own = offset(p, d)
            if kind == "qk":
                qb, tile = divmod(k, 3)
                rows = (TILES[tile][1] - TILES[tile][0]) * HD
                act.wait_ge(remain.sem, remain.at(own.n, k + 1))
                nc.scalar.copy(pieces[0:rows, tile, 1, CHUNK * qb:CHUNK * qb + CHUNK],
                               left[0:rows, k % 2, :]).then_inc(second.sem, 1)
            elif kind == "out":
                act.wait_ge(t1_done.sem, t1_done.at(own.n, k + 1))
                if not (isinstance(own.n, int) and own.n == 0 and k == 0):
                    act.wait_ge(sq_done.sem, sq_done.at(own.n, k))
                nc.scalar.activation(sqr[:, :], t1[:, k % 3, :], ACT.Square,
                                     accum_out=mo[:, own.h, 6 + k:7 + k]).then_inc(sq_done.sem, 1)

        def exponentials(p, t, pair):
            for x in range(2 * pair, 2 * pair + 2):
                k = QUAD * t + x
                act.wait_ge(score_made.sem, score_made.at(p.n, k + 1))
                if x == 0 and not (isinstance(p.n, int) and p.n == 0 and t < 2):
                    act.wait_ge(valued.sem, valued.at(p.n, t - 1))
                nc.scalar.activation(ex[:, k % RING, :], sc[x][:, :], ACT.Exp, scale=scale).then_inc(exped.sem, 1)

        def outputs(p, g):
            act.wait_ge(valued.sem, valued.at(p.n, 8 * g + 8))
            if not (isinstance(p.n, int) and p.n == 0 and g == 0):
                act.wait_ge(o_normed.sem, o_normed.at(p.n, g))
            nc.scalar.copy(oc[:, :], po[:, :]).then_inc(o_copied.sem, 1)

        def unit(p, which):
            for t in range(STEPS):
                if 0 in which:
                    exponentials(p, t, 0)
                if t == 0 and -1 in which:
                    outputs(p.to(-1), 3)
                elif t and t % 8 == 0 and 0 in which:
                    outputs(p, t // 8 - 1)
                if 0 in which:
                    exponentials(p, t, 1)
                late_task(p, t - 1, which)
                task(p, t, which)

        run_units(act, units, unit)

    @block.vector
    def _(dve):
        step = [0]

        def link(ins):
            step[0] += 1
            ins.then_inc(chain, 1)
            dve.wait_ge(chain, step[0])

        dve.sem_inc(maxed.sem, maxed.base)
        dve.wait_ge(fixed, 16 * 7)
        nc.vector.memset(ks[96:128, :, :, :], 1.0)
        nc.vector.memset(qs[96:128, :, :, :], 0.0)
        link(nc.vector.memset(va[:, :, :, :, :], 0.0))
        link(nc.vector.memset(va[:, :, :, :, HD:HD + 1], 1.0))
        nc.vector.tensor_copy(ident_b[:, :], ident[:, :]).then_inc(prepared, 1)

        def task(p, t, which):
            if t not in TASKS or TASKS[t][0] not in which:
                return
            d, kind, k = TASKS[t]
            own = offset(p, d)
            n = own.n
            if kind == "qk":
                qb, tile = divmod(k, 3)
                rows = (TILES[tile][1] - TILES[tile][0]) * HD
                dve.wait_ge(lead.sem, lead.at(n, k + 1))
                if not (isinstance(n, int) and n == 0 and k < 2):
                    dve.wait_ge(third.sem, third.at(n, k - 1))
                nc.vector.tensor_tensor(left[0:rows, k % 2, :], pm[0:rows, :],
                                        pieces[0:rows, tile, 0, CHUNK * qb:CHUNK * qb + CHUNK],
                                        ALU.subtract).then_inc(remain.sem, 1)
            elif kind == "turn":
                dve.wait_ge(o_turned.sem, o_turned.at(n, k + 1))
                nc.vector.reciprocal(rz[:, :].rearrange("p (b h) -> p b h", h=QUAD),
                                     pm[:, :].rearrange("p (b h e) -> p b h e", h=QUAD, e=32)[:, :, :, HD]).then_inc(z_inv.sem, 1)
                dve.wait_ge(z_inv.sem, z_inv.at(n, k + 1))
                nc.vector.tensor_copy(rb[:, :, :, :].rearrange("p b h e -> p (b h) e"),
                                      rz[:, :].unsqueeze(2).to_broadcast([128, BLK * QUAD, 32])).then_inc(rb_ready.sem, 1)
            elif kind == "back":
                dve.wait_ge(rb_turned.sem, rb_turned.at(n, k + 1))
                nc.vector.tensor_tensor(on[:, k, :], pm[:, :], oc[:, :], ALU.mult).then_inc(o_normed.sem, 1)
            elif kind == "out":
                qb, i = divmod(k, 3)
                dve.wait_ge(out_made.sem, out_made.at(n, k + 1))
                if k == 0:
                    dve.wait_ge(tw_in[own.h].sem, tw_in[own.h].at(own.m, 48))
                    dve.wait_ge(mo_stored[own.h].sem, mo_stored[own.h].at(own.m, 0))
                dve.wait_ge(t1_stored[i].sem, t1_stored[i].at(n, 16 * qb))
                if not (isinstance(n, int) and n == 0 and qb == 0):
                    dve.wait_ge(sq_done.sem, sq_done.at(n, k - 2))
                first = (CROWS * qb + i) * IMG
                nc.vector.scalar_tensor_tensor(out=t1[:, i, :], in0=pm[0:R, :], scalar=1.0,
                                               in1=tw[:, own.h, first:first + CHUNK], op0=ALU.mult, op1=ALU.add,
                                               accum_out=mo[:, own.h, k:k + 1]).then_inc(t1_done.sem, 1)

        def maximum(p, t, x):
            k = 4 * t + x
            dve.wait_ge(max_made.sem, max_made.at(p.n, k + 1))
            nc.vector.tensor_reduce(big[:, x % 2, k // 2:k // 2 + 1], mp[x % 2][:, :],
                                    AX_X, ALU.max).then_inc(maxed.sem, 1)

        def negate(p, quad):
            n = p.n
            halves_of = [big[:, half, 32 * quad:32 * quad + 32] for half in range(2)]
            dve.wait_ge(maxed.sem, maxed.at(n, 64 * quad + 64))
            nc.vector.tensor_tensor(top[:, :], halves_of[0], halves_of[1], ALU.max).then_inc(m0.sem, 1)
            dve.wait_ge(m0.sem, m0.at(n, quad + 1))
            if not (isinstance(n, int) and n == 0 and quad == 0):
                dve.wait_ge(neg_turned.sem, neg_turned.at(n, quad))
            nc.vector.tensor_scalar(mparts[:, 0, :], top[:, :], -1.0, None, ALU.mult).then_inc(m1.sem, 1)
            dve.wait_ge(m1.sem, m1.at(n, quad + 1))
            nc.vector.scalar_tensor_tensor(out=mleft[:, 0, :], in0=top[:, :], scalar=-1.0, in1=mparts[:, 0, :],
                                           op0=ALU.mult, op1=ALU.subtract).then_inc(m2.sem, 1)
            dve.wait_ge(m2.sem, m2.at(n, quad + 1))
            nc.vector.tensor_copy(mparts[:, 1, :], mleft[:, 0, :]).then_inc(m3.sem, 1)
            dve.wait_ge(m3.sem, m3.at(n, quad + 1))
            nc.vector.tensor_tensor(mparts[:, 2, :], mleft[:, 0, :], mparts[:, 1, :], ALU.subtract).then_inc(negated.sem, 1)

        def unit(p, which):
            for t in range(STEPS):
                for x in range(4):
                    if 1 in which:
                        maximum(p.to(1), t, x)
                    if x == 1:
                        task(p, t - 1, which)
                if 1 in which and t % 16 == 15:
                    negate(p.to(1), t // 16)

        run_units(dve, units, unit)


CHUNKS = PIX // CHUNK
ROWS3 = 3 * C


def fold_phase(nc, ctx, sems, mixed, moments, total, result, w_1, w_2, b_1, consts):
    units = mixed.shape[0]
    samples = units // 4

    def sb(n, shape, dt=F32):
        return ctx.enter_context(nc.sbuf_tensor(f"f_{n}", shape, dt))

    def sem(n):
        sems.append(nc.alloc_semaphore(f"f_{n}"))
        return sems[-1]

    t = sb("t", [ROWS3, 2, 3, PAD * IMG])
    hidden = sb("hidden", [ROWS3, PAD * IMG])
    three = sb("three", [ROWS3, 4, CHUNK])
    two = sb("two", [ROWS3, CHUNK])
    u = sb("u", [ROWS3, CHUNKS, CROWS, PAD])
    x1 = sb("x1", [128, 2, 2, CHUNK])
    out = sb("out", [128, 2, 2, CHUNK])
    w1 = sb("w1", [ROWS3, 3, HID])
    w2 = sb("w2", [ROWS3, 3, ROWS3])
    b1 = sb("b1", [HID, 1])
    sel = sb("sel", [ROWS3, 3, C])
    mom = sb("mom", [ROWS3, units, 12])
    ones = sb("ones", [ROWS3, ROWS3])
    mean_of = sb("mean_of", [ROWS3, ROWS3])
    m6 = sb("m6", [ROWS3, units * 2])
    m2 = sb("m2", [ROWS3, samples, 2])
    avg = sb("avg", [ROWS3, samples * 2])
    colsum = sb("colsum", [HID, 1])
    var = sb("var", [ROWS3, samples])
    lnv = sb("lnv", [ROWS3, samples])
    root = sb("root", [ROWS3, samples])
    work = sb("work", [ROWS3, samples])
    rstd = sb("rstd", [ROWS3, samples])
    bias = sb("bias", [ROWS3, samples])
    coef = sb("coef", [ROWS3, 2, 2])
    ph = [ctx.enter_context(nc.psum_tensor(f"f_ph{i}", [128, CHUNK], F32)) for i in range(2)]
    pw = [ctx.enter_context(nc.psum_tensor(f"f_pw{i}", [128, CHUNK], F32)) for i in range(2)]
    pf = [ctx.enter_context(nc.psum_tensor(f"f_pf{i}", [128, CHUNK], F32)) for i in range(2)]
    px = ctx.enter_context(nc.psum_tensor("f_px", [128, CHUNK], F32))

    fixed = sem("fixed")
    chain = sem("chain")
    moments_ready = sem("moments_ready")
    averaged = sem("averaged")
    var_ready = sem("var_ready")
    root_ready = sem("root_ready")
    prepared = sem("prepared")
    coef_ready = Signal(sem("coef_ready"), 2)
    loaded = [Signal(sem(f"loaded{h}"), 16 * 7) for h in range(2)]
    h_made = Signal(sem("h_made"), CHUNKS)
    h_done = Signal(sem("h_done"), CHUNKS, 1)
    w_made = Signal(sem("w_made"), CHUNKS)
    paired = Signal(sem("paired"), CHUNKS, 1)
    summed = Signal(sem("summed"), CHUNKS, 1)
    u_done = Signal(sem("u_done"), CHUNKS, 1)
    folded = Signal(sem("folded"), 2, 1)
    out_done = Signal(sem("out_done"), 2, 1)
    stored = [Signal(sem(f"stored{h}"), 64, 1) for h in range(2)]

    block = ctx.enter_context(nc.Block())

    def in_pairs(engine, sample, peeled=False):
        if peeled:
            sample(Pass(0, 0, 0))
            sample(Pass(1, 1, 0))
        with engine.Fori(int(peeled), samples // 2) as i:
            sample(Pass(2 * i, 0, i))
            sample(Pass(2 * i + 1, 1, i))

    @block.sync
    def _(sp):
        for to, src in ((w1[:, :, :], w_1), (w2[:, :, :], w_2), (b1[:, :], b_1),
                        (sel[:, :, :], consts["sel"]), (mom[:, :, :], moments)):
            sp.dma_start(to, src).then_inc(fixed, 16)

        def load(p):
            for i in range(3):
                src = mixed[bass.ds(4 * p.n, 4), i, :, :].rearrange("u p x -> p u x")
                sp.dma_start(t[:, p.h, i, IMG:IMG + PIX].rearrange("p (u x) -> p u x", u=4),
                             src).then_inc(loaded[p.h].sem, 16)
            image = total[bass.ds(C * p.n, C), :].rearrange("c (q l x) -> c l q x", l=LANES, x=CHUNK)
            for l in range(LANES):
                sp.dma_start(x1[C * l:C * l + C, p.h, :, :], image[:, l, :, :]).then_inc(loaded[p.h].sem, 16)

        def store(p):
            sp.wait_ge(out_done.sem, out_done.at(p.n, 2))
            image = result[bass.ds(C * p.n, C), :].rearrange("c (q l x) -> c l q x", l=LANES, x=CHUNK)
            for l in range(LANES):
                sp.dma_start(image[:, l, :, :], out[C * l:C * l + C, p.h, :, :]).then_inc(stored[p.h].sem, 16)

        sp.wait_ge(prepared, 1)
        load(Pass(0, 0, 0))
        load(Pass(1, 1, 0))
        if samples > 2:
            with sp.Fori(0, samples // 2 - 1) as i:
                for h in range(2):
                    store(Pass(2 * i + h, h, i))
                    load(Pass(2 * i + 2 + h, h, i + 1))
        for h in range(2):
            store(Pass(samples - 2 + h, h, samples // 2 - 1))
        for h in range(2):
            sp.wait_ge(stored[h].sem, stored[h].at(samples // 2, 0))

    @block.tensor
    def _(pe):
        pe.wait_ge(fixed, 16 * 5)
        pe.wait_ge(moments_ready, 1)
        for i in range(3):
            pe.matmul(px[0:HID, 64:65], w1[:, i, :], ones[:, 0:1], start=i == 0, stop=i == 2)
        pe.matmul(px[0:ROWS3, 0:2 * samples], mean_of[:, :], m2[:, :, :].rearrange("p s k -> p (s k)"),
                  start=True, stop=True).then_inc(averaged, 1)
        pe.sem_inc(folded.sem, folded.base)

        def hide(p, k):
            if k == 0:
                pe.wait_ge(loaded[p.h].sem, loaded[p.h].at(p.m, 16 * 7))
            pe.wait_ge(h_done.sem, h_done.at(p.n, k - 1))
            for i in range(3):
                first = (CROWS * k + 1) * IMG
                last = pe.matmul(ph[k % 2][0:HID, :], w1[:, i, :], t[:, p.h, i, first:first + CHUNK],
                                 start=i == 0, stop=i == 2)
            last.then_inc(h_made.sem, 1)

        def unhide(p, k):
            pe.wait_ge(h_done.sem, h_done.at(p.n, min(k + 2, CHUNKS)))
            pe.wait_ge(u_done.sem, u_done.at(p.n, k - 1))
            for i in range(3):
                first = (CROWS * k + 2 - i) * IMG
                last = pe.matmul(pw[k % 2][0:ROWS3, :], w2[:, i, :], hidden[:, first:first + CHUNK],
                                 start=i == 0, stop=i == 2)
            last.then_inc(w_made.sem, 1)

        def fold(p, q):
            pe.wait_ge(u_done.sem, u_done.at(p.n, LANES * (q + 1)))
            pe.wait_ge(out_done.sem, out_done.at(p.n, q - 1))
            for j in range(3):
                for l in range(LANES):
                    last = pe.matmul(pf[q][C * l:C * l + C, :].rearrange("p (a b) -> p a b", b=IMG), sel[:, j, :],
                                     u[:, LANES * q + l, :, 2 - j:2 - j + IMG], start=j == 0, stop=j == 2,
                                     tile_position=(0, C * l))
            last.then_inc(folded.sem, 1)

        def sample(p):
            for k in range(CHUNKS + 2):
                if k < CHUNKS:
                    hide(p, k)
                if k == 2 and not (isinstance(p.n, int) and p.n == 0):
                    fold(p.to(-1), 1)
                if k == CHUNKS - 1:
                    fold(p, 0)
                if k >= 2:
                    unhide(p, k - 2)

        pe.wait_ge(prepared, 1)
        in_pairs(pe, sample, peeled=True)
        fold(Pass(samples - 1, 1, samples // 2 - 1), 1)

    @block.scalar
    def _(act):
        nc.scalar.preload_act_table_set(EXP_LN)
        act.sem_inc(h_done.sem, h_done.base)
        act.wait_ge(var_ready, 1)
        nc.scalar.activation(lnv[:, :], var[:, :], ACT.Ln).then_inc(root_ready, 1)
        act.wait_ge(root_ready, 1)
        nc.scalar.activation(root[:, :], lnv[:, :], ACT.Exp, scale=-0.5).then_inc(root_ready, 1)
        act.wait_ge(prepared, 1)

        def sample(p):
            for k in range(CHUNKS):
                if k == 0:
                    act.wait_ge(coef_ready.sem, coef_ready.at(p.n, 2))
                act.wait_ge(h_made.sem, h_made.at(p.n, k + 1))
                first = (CROWS * k + 1) * IMG
                nc.scalar.activation(hidden[0:HID, first:first + CHUNK], ph[k % 2][0:HID, :], ACT.Relu,
                                     scale=coef[0:HID, p.h, 0:1], bias=coef[0:HID, p.h, 1:2]).then_inc(h_done.sem, 1)

        in_pairs(act, sample)

    @block.gpsimd
    def _(pool):
        pool.sem_inc(paired.sem, paired.base)
        pool.sem_inc(summed.sem, summed.base)

        def sample(p):
            for k in range(CHUNKS):
                rows = [slice((CROWS * k + 2 - i) * IMG, (CROWS * k + 2 - i) * IMG + CHUNK) for i in range(3)]
                if k == 0:
                    pool.wait_ge(loaded[p.h].sem, loaded[p.h].at(p.m, 16 * 7))
                pool.wait_ge(summed.sem, summed.at(p.n, k))
                nc.gpsimd.tensor_tensor(two[:, :], t[:, p.h, 0, rows[0]], t[:, p.h, 1, rows[1]],
                                        ALU.add).then_inc(paired.sem, 1)
                pool.wait_ge(paired.sem, paired.at(p.n, k + 1))
                pool.wait_ge(u_done.sem, u_done.at(p.n, k - 3))
                nc.gpsimd.tensor_tensor(three[:, k % 4, :], two[:, :], t[:, p.h, 2, rows[2]],
                                        ALU.add).then_inc(summed.sem, 1)

        in_pairs(pool, sample)

    @block.vector
    def _(dve):
        step = [0]

        def link(ins):
            step[0] += 1
            ins.then_inc(chain, 1)
            dve.wait_ge(chain, step[0])

        dve.sem_inc(u_done.sem, u_done.base)
        dve.sem_inc(out_done.sem, out_done.base)
        link(nc.vector.memset(ones[:, :], 1.0))
        link(nc.vector.memset(mean_of[:, :], 1.0 / (PIX * DIM)))
        for h in range(2):
            for i in range(3):
                edges = t[:, h, i, :].rearrange("p (a b) -> p a b", b=IMG)
                link(nc.vector.memset(edges[:, 0:PAD:PAD - 1, :], 0.0))
        link(nc.vector.memset(hidden[:, :], 0.0))
        link(nc.vector.memset(hidden[64:ROWS3, IMG:IMG + PIX], 1.0))
        link(nc.vector.memset(u[:, :, :, :], 0.0))
        dve.wait_ge(fixed, 16 * 5)
        link(nc.vector.tensor_reduce(m6[:, :], mom[:, :, :].rearrange("p u (k x) -> p (u k) x", x=6), AX_X, ALU.add))
        nc.vector.tensor_reduce(m2[:, :, :], m6[:, :].rearrange("p (s u k) -> p s k u", u=4, k=2), AX_X,
                                ALU.add).then_inc(moments_ready, 1)
        dve.wait_ge(averaged, 1)
        link(nc.vector.tensor_copy(avg[:, :], px[0:ROWS3, 0:2 * samples]))
        link(nc.vector.tensor_copy(colsum[:, :], px[0:HID, 64:65]))
        mean, square = (avg[:, :].rearrange("p (s k) -> p s k", k=2)[:, :, k] for k in range(2))
        link(nc.vector.tensor_tensor(work[:, :], mean, mean, ALU.mult))
        link(nc.vector.tensor_tensor(work[:, :], square, work[:, :], ALU.subtract))
        nc.vector.tensor_scalar(var[:, :], work[:, :], LN_EPS, None, ALU.add).then_inc(var_ready, 1)
        dve.wait_ge(root_ready, 2)
        link(nc.vector.tensor_tensor(work[:, :], root[:, :], root[:, :], ALU.mult))
        link(nc.vector.tensor_tensor(work[:, :], work[:, :], var[:, :], ALU.mult))
        link(nc.vector.tensor_scalar(work[:, :], work[:, :], -0.5, 1.5, ALU.mult, ALU.add))
        link(nc.vector.tensor_tensor(rstd[:, :], work[:, :], root[:, :], ALU.mult))
        link(nc.vector.tensor_tensor(work[:, :], rstd[:, :], mean, ALU.mult))
        link(nc.vector.tensor_scalar(bias[0:HID, :], work[0:HID, :], colsum[:, 0:1], -1.0, ALU.mult, ALU.mult))
        nc.vector.tensor_scalar(bias[0:HID, :], bias[0:HID, :], b1[:, 0:1], None, ALU.add).then_inc(prepared, 1)
        dve.wait_ge(prepared, 1)

        def finish(p, q):
            if q == 0:
                dve.wait_ge(stored[p.h].sem, stored[p.h].at(p.m, 0))
            dve.wait_ge(folded.sem, folded.at(p.n, q + 1))
            nc.vector.tensor_tensor(out[:, p.h, q, :], pf[q][:, :], x1[:, p.h, q, :], ALU.add).then_inc(out_done.sem, 1)

        def sample(p):
            for k, of in enumerate((rstd, bias)):
                nc.vector.tensor_copy(coef[0:HID, p.h, k:k + 1], of[0:HID, bass.ds(p.n, 1)]).then_inc(coef_ready.sem, 1)
            for k in range(CHUNKS):
                dve.wait_ge(w_made.sem, w_made.at(p.n, k + 1))
                dve.wait_ge(summed.sem, summed.at(p.n, k + 1))
                if k % LANES == 0:
                    dve.wait_ge(folded.sem, folded.at(p.n, k // LANES - 1))
                nc.vector.tensor_tensor(u[:, k, :, 1:IMG + 1], pw[k % 2][0:ROWS3, :].rearrange("p (a b) -> p a b", b=IMG),
                                        three[:, k % 4, :].rearrange("p (a b) -> p a b", b=IMG),
                                        ALU.add).then_inc(u_done.sem, 1)
                if k == 0 and not (isinstance(p.n, int) and p.n == 0):
                    finish(p.to(-1), 1)
                if k == CHUNKS - 2:
                    finish(p, 0)

        for h in range(2):
            dve.sem_inc(stored[h].sem, stored[h].base)
        in_pairs(dve, sample, peeled=True)
        finish(Pass(samples - 1, 1, samples // 2 - 1), 1)


def program(nc, x, w_sum, w_vote, w_r, w_qkv, w_p, w_1, b_1, w_2, ident, pick, pairs, sample, count, sel, result):
    batch = x.shape[0]
    rows = x.rearrange("b c h w -> (b c) (h w)")

    def scratch(name, shape):
        return nc.dram_tensor(name, shape, F32, kind="Internal").ap()

    first = scratch("first", [2 * batch, C, HALF])
    routed = scratch("routed", [2 * batch, C, PIX // 2])
    second = scratch("second", [2 * batch, C, HALF])
    layered = scratch("layered", [2 * batch, C, HALF])
    total = scratch("total", [batch * C, PIX])
    mixed = scratch("mixed", [4 * batch, 3, 3 * C, UNIT])
    moments = scratch("moments", [3 * C, 4 * batch, 12])

    def phase(body, *args):
        sems = []
        with ExitStack() as ctx:
            body(nc, ctx, sems, *args)
        nc.clear_and_free_semaphores(sems)
        nc.all_engine_barrier()

    phase(norm_phase, "n1", rows, None, dict(pairs=pairs), first)
    phase(routing_phase, first, routed, w_sum, w_vote, dict(ident=ident, pick=pick))
    phase(norm_phase, "n2", rows, routed, dict(pairs=pairs, sample=sample, count=count), second, layered, total)
    phase(attention_phase, second, layered, mixed, moments, w_r, w_qkv, w_p, dict(ident=ident))
    phase(fold_phase, mixed, moments, total, result.rearrange("b c h w -> (b c) (h w)"), w_1, w_2, b_1,
          dict(sel=sel))


def lay_out(inputs):
    f = np.float32
    w = inputs["L0_conv_weight"]
    w_sum = np.zeros((CAPS, CAPS, CLEN, TAPS, CAPS, CLEN), f)
    for o in range(CAPS):
        w_sum[o, :, :, :, o, :] = w[o].transpose(0, 4, 1, 2, 3).reshape(CAPS, CLEN, TAPS, CLEN)
    w_sum = w_sum.reshape(128, TAPS, C)
    w_p = np.zeros((QUADS, QUAD, 32, 3, 3, C), f)
    w_p[:, :, :HD] = inputs["L1_conv_Wp"].reshape(C, 3, 3, QUADS, QUAD, HD).transpose(3, 4, 5, 1, 2, 0)
    w_p[0, 0, HD] = inputs["L1_conv_bp"].reshape(C, 3, 3).transpose(1, 2, 0)
    w_2 = np.zeros((3 * C, 3, 3, C), f)
    w_2[:HID] = inputs["L1_conv_W2"].reshape(C, 3, 3, HID).transpose(3, 1, 2, 0)
    w_2[HID] = inputs["L1_conv_b2"].reshape(C, 3, 3).transpose(1, 2, 0)
    pick = np.zeros((128, 2, C), f)
    for p in range(128):
        for t in range(2):
            pick[p, t, 16 * t + p // CLEN] = 1
    times = np.full(IMG, 3, f)
    times[[0, -1]] = 2
    return dict(
        x=inputs["x"], w_sum=w_sum, w_vote=w_sum.transpose(2, 1, 0).reshape(C, TAPS * 128),
        w_r=inputs["L1_conv_Wr"].reshape(C2, C, 3, 3).transpose(0, 2, 3, 1).reshape(C2, 3, 3 * C),
        w_qkv=inputs["L1_conv_Wqkv"].T, w_p=w_p.reshape(QUADS, 128, 3, 3 * C),
        w_1=inputs["L1_conv_W1"].reshape(HID, C, 3, 3).transpose(3, 1, 2, 0).reshape(3 * C, 3, HID),
        b_1=inputs["L1_conv_b1"].reshape(HID, 1), w_2=w_2.reshape(3 * C, 3, 3 * C),
        ident=np.eye(128, dtype=f), pick=pick,
        pairs=np.kron(np.eye(64, dtype=f), np.full((2, 2), 0.5, f)),
        sample=np.kron(np.eye(4, dtype=f), np.full((C, C), 1 / (PIX * DIM), f)),
        count=np.outer(times, times).reshape(1, PIX),
        sel=np.eye(3 * C, dtype=f).reshape(3 * C, 3, C))


def kernel(**inputs):
    import concourse.bacc as _bacc
    from concourse.bass_utils import run_bass_kernel_spmd as _run

    nc = _bacc.Bacc("TRN2", target_bir_lowering=False, num_devices=1)
    arrays, args = {}, {}
    for name, a in lay_out({k: np.asarray(v) for k, v in inputs.items()}).items():
        a = np.ascontiguousarray(a)
        arrays[f"in_{name}"] = a
        args[name] = nc.dram_tensor(f"in_{name}", a.shape, mybir.dt.from_np(a.dtype), kind="ExternalInput").ap()
    shape = arrays["in_x"].shape
    args["result"] = nc.dram_tensor("out", shape, F32, kind="ExternalOutput").ap()
    program(nc, **args)
    r = _run(nc, [arrays], core_ids=[0])
    return r.results[0]["out"]
```
